# Optimizing a Trainium2 kernel written in Bass

```python
import numpy as np
import jax
import jax.numpy as jnp

def _softmax(x, axis=-1):
    return jax.nn.softmax(x, axis=axis)

def _gelu(x):
    return jax.nn.gelu(x, approximate=True)

def _silu(x):
    return jax.nn.silu(x)

def _sigmoid(x):
    return jax.nn.sigmoid(x)

def _layernorm(x, axis=-1, eps=1e-05):
    m = jnp.mean(x, axis=axis, keepdims=True)
    v = jnp.var(x, axis=axis, keepdims=True)
    return (x - m) / jnp.sqrt(v + eps)

def _scatter_add(tgt, idx, src, axis=0):
    return tgt.at[idx].add(src)

def _segment_sum(src, seg, n):
    return jax.ops.segment_sum(src, seg, n)
kernel_name = 'mk_prb_d1_jaxref_r4_09bffb'

def setup_inputs(seed: int=0):
    np.random.seed(seed)
    _w = jnp.asarray

    def _L0_attn_setup():
        import jax, jax.numpy as jnp
        import numpy as np
        import math
        N_EMBD = 512
        N_HEADS = 16
        HEAD_DIM = N_EMBD // N_HEADS
        CTX = 512

        def alibi_bias(seq_len: int, n_heads: int) -> jnp.ndarray:
            i = jnp.arange(seq_len)[:, None]
            j = jnp.arange(seq_len)[None, :]
            pos = jnp.where(j <= i, (j - i).astype(jnp.float32), 0.0)
            slopes = 2.0 ** (-8.0 / jnp.arange(1, n_heads + 1, dtype=jnp.float32))
            return slopes[:, None, None] * pos[None, :, :]

        def causal_mask(seq_len: int) -> jnp.ndarray:
            i = jnp.arange(seq_len)[:, None]
            j = jnp.arange(seq_len)[None, :]
            return jnp.where(j > i, -jnp.inf, 0.0).astype(jnp.float32)
        key = jax.random.key(seed)
        k_x, k_qkv, k_o = jax.random.split(key, 3)
        scale = 1.0 / math.sqrt(N_EMBD)
        x = jax.random.normal(k_x, (2, CTX, N_EMBD), dtype=jnp.float32)
        W_qkv = jax.random.normal(k_qkv, (N_EMBD, 3 * N_EMBD), dtype=jnp.float32) * scale
        W_o = jax.random.normal(k_o, (N_EMBD, N_EMBD), dtype=jnp.float32) * scale
        return {'x': x, 'W_qkv': W_qkv, 'W_o': W_o}
    _L0_attn_in = _L0_attn_setup()

    def _L0_ffn_setup():
        import jax, jax.numpy as jnp
        import numpy as np
        B, S, H, E = (4, 512, 512, 8)
        key = jax.random.key(seed)
        k_x, k_wg, k_w, k_b = jax.random.split(key, 4)
        x = jax.random.normal(k_x, (B, S, H), dtype=jnp.float32)
        wg = jax.random.normal(k_wg, (H, E), dtype=jnp.float32) * (1.0 / np.sqrt(H))
        W = jax.random.normal(k_w, (E, H, H), dtype=jnp.float32) * (1.0 / np.sqrt(H))
        b = jax.random.normal(k_b, (E, H), dtype=jnp.float32) * 0.01
        return {'x': x, 'wg': wg, 'W': W, 'b': b}
    _L0_ffn_in = _L0_ffn_setup()
    _d = {'L0_attn_x': _L0_attn_in['x'], 'L0_attn_W_qkv': _L0_attn_in['W_qkv'], 'L0_attn_W_o': _L0_attn_in['W_o'], 'L0_ffn_wg': _L0_ffn_in['wg'], 'L0_ffn_W': _L0_ffn_in['W'], 'L0_ffn_b': _L0_ffn_in['b']}
    _x0 = _d['L0_attn_x']
    _d['L0_attn_x'] = jax.random.normal(jax.random.fold_in(jax.random.key(seed), 1), (2, 2048, 512), dtype=_x0.dtype)
    del _x0
    return _d

def reference(L0_attn_x, L0_attn_W_qkv, L0_attn_W_o, L0_ffn_wg, L0_ffn_W, L0_ffn_b):

    def _L0_attn_ref(x, W_qkv, W_o):
        import jax, jax.numpy as jnp
        import numpy as np
        import math
        N_EMBD = 512
        N_HEADS = 16
        HEAD_DIM = N_EMBD // N_HEADS
        CTX = 512

        def alibi_bias(seq_len: int, n_heads: int) -> jnp.ndarray:
            i = jnp.arange(seq_len)[:, None]
            j = jnp.arange(seq_len)[None, :]
            pos = jnp.where(j <= i, (j - i).astype(jnp.float32), 0.0)
            slopes = 2.0 ** (-8.0 / jnp.arange(1, n_heads + 1, dtype=jnp.float32))
            return slopes[:, None, None] * pos[None, :, :]

        def causal_mask(seq_len: int) -> jnp.ndarray:
            i = jnp.arange(seq_len)[:, None]
            j = jnp.arange(seq_len)[None, :]
            return jnp.where(j > i, -jnp.inf, 0.0).astype(jnp.float32)
        bsz, seq_len, n_embd = x.shape
        qkv = jnp.einsum('bsd,de->bse', x, W_qkv)
        q, k, v = jnp.split(qkv, 3, axis=-1)

        def to_heads(t):
            return t.reshape(bsz, seq_len, N_HEADS, HEAD_DIM).transpose(0, 2, 1, 3)
        q, k, v = (to_heads(q), to_heads(k), to_heads(v))
        attn = jnp.einsum('bhqd,bhkd->bhqk', q, k) / math.sqrt(HEAD_DIM)
        attn = attn + alibi_bias(seq_len, N_HEADS)[None] + causal_mask(seq_len)[None, None]
        attn = jax.nn.softmax(attn, axis=-1)
        y = jnp.einsum('bhqk,bhkd->bhqd', attn, v)
        y = y.transpose(0, 2, 1, 3).reshape(bsz, seq_len, n_embd)
        return jnp.einsum('bsd,de->bse', y, W_o)

    def _L0_ffn_ref(x, wg, W, b):
        import jax, jax.numpy as jnp
        import numpy as np
        B, S, H, E = (4, 512, 512, 8)
        Bv, Sv, Hv = x.shape
        Ev = W.shape[0]
        xt = x.reshape(-1, Hv)
        logits = xt @ wg
        probs = jax.nn.softmax(logits, axis=-1)
        idx = jnp.argmax(probs, axis=-1)
        gate = jnp.take_along_axis(probs, idx[:, None], axis=1)
        onehot = jax.nn.one_hot(idx, Ev, dtype=x.dtype)
        expert_out = jnp.einsum('nh,eoh->neo', xt, W) + b[None, :, :]
        combine = onehot * gate
        out = jnp.einsum('ne,neo->no', combine, expert_out)
        return out.reshape(Bv, Sv, Hv)
    x = L0_attn_x
    xn = _layernorm(x, axis=-1)
    x = x + _L0_attn_ref(xn, L0_attn_W_qkv, L0_attn_W_o) + _L0_ffn_ref(xn, L0_ffn_wg, L0_ffn_W, L0_ffn_b)
    return x

_drawn_inputs = setup_inputs


def setup_inputs(seed=0):
    import zlib

    import numpy as np

    out = dict(_drawn_inputs(seed))
    spreads = {}
    factors = {'L0_ffn_b': 8.0}
    for name, (base, spread) in spreads.items():
        noise = np.random.default_rng([zlib.crc32(name.encode()), seed]).standard_normal(out[name].shape)
        drawn = base * np.exp(spread * noise) if base else spread * noise
        out[name] = jnp.asarray(drawn.astype(out[name].dtype))
    for name, factor in factors.items():
        out[name] = (out[name] * factor).astype(out[name].dtype)
    return out
```

```python
from contextlib import ExitStack

import numpy as np

import concourse.bass as bass
from concourse import mybir
from concourse.alu_op_type import AluOpType as ALU

F32 = mybir.dt.float32
F32R = mybir.dt.float32r
BF16 = mybir.dt.bfloat16
I32 = mybir.dt.int32
ACT = mybir.ActivationFunctionType
AX = mybir.AxisListType

P = 128
B, S, D = 2, 2048, 512
H, DH = 16, 32
E = 8
N = B * S
CH = 512
NCH = N // CH
TPC = CH // P
NT = N // P
KC = D // P
HG = P // DH
G = B * H // HG
GB = H // HG
QT = S // P
QC = S // CH
SLOT_TILES = NT + E - 1
SLOTS = (SLOT_TILES + 1) * P
EPS = 1e-5
NEG = -1e30
SCALE = float(np.float32(1.0) / np.sqrt(np.float32(DH)))
SLOPES = [float(np.float32(2.0) ** (np.float32(-8.0) / np.float32(i))) for i in range(1, H + 1)]

ROW_ALIBI = 3 * DH
ROW_MAX = ROW_ALIBI + 2
ROWS = ROW_MAX + 2

ROUNDS = [(c, jb) for c in range(QC) for jb in range(TPC * (c + 1))]
NR = len(ROUNDS)
MAX_UNITS = [(i, kc, hh) for i in range(QT) for kc in range(i // TPC + 1) for hh in range(HG)]
NMU = len(MAX_UNITS)
NSU = NR * HG
MAX_FROM, MAX_TO = 8, 36
FOLD_AT = 37
S_BANKS, M_BANKS, P_SLOTS = 3, 3, 4
PAIR_OF = {}
for _r, (_c, _jb) in enumerate(ROUNDS):
    if _jb < TPC * _c:
        PAIR_OF[_r] = len(PAIR_OF) // 2
NPAIR = len(PAIR_OF) // 2
PAIR_LAST = {p: r for r, p in PAIR_OF.items()}
LAST_ROUND = [max(r for r, (cc, _) in enumerate(ROUNDS) if cc == c) for c in range(QC)]


class Memory:
    pass


def max_units_of(r):
    if not MAX_FROM <= r < MAX_TO:
        return []
    w = MAX_TO - MAX_FROM
    return range(NMU * (r - MAX_FROM) // w, NMU * (r - MAX_FROM + 1) // w)


def wait_past(eng, sem, count):
    if not isinstance(count, int) or count > 0:
        eng.wait_ge(sem, count)


def earlier_user(u, ring, per_group):
    if u >= ring:
        return 0, u - ring
    return 1, max(v for v in range(per_group) if v % ring == u % ring)


def prenorm_alibi_attention_plus_top1_experts(nc, x, w_qkv, w_o, w_g, w_e, b_e, out):
    m = Memory()
    m.x, m.out = x.rearrange("b s d -> (b s) d"), out.rearrange("b s d -> (b s) d")
    m.w_qkv, m.w_o, m.w_g, m.w_e, m.b_e = w_qkv, w_o, w_g, w_e, b_e

    m.q_hi_d = nc.dram_tensor("q_hi_d", [G, P, S], F32).ap()
    m.q_lo_d = nc.dram_tensor("q_lo_d", [G, P, S], F32).ap()
    m.k_hi_d = nc.dram_tensor("k_hi_d", [G, P, S], F32).ap()
    m.k_lo_d = nc.dram_tensor("k_lo_d", [G, P, S], F32).ap()
    m.v_d = nc.dram_tensor("v_d", [N, D], F32).ap()
    m.xn_d = nc.dram_tensor("xn_d", [N, D], F32).ap()
    m.y_d = nc.dram_tensor("y_d", [G, P, S], F32).ap()
    m.slot_x_d = nc.dram_tensor("slot_x_d", [SLOTS, D], F32).ap()
    m.slot_y_d = nc.dram_tensor("slot_y_d", [SLOT_TILES * P, D], F32).ap()
    m.k_rows_d = nc.dram_tensor("k_rows_d", [4, H, S], F32).ap()
    m.q_rows_d = nc.dram_tensor("q_rows_d", [6, HG, S], F32).ap()

    with ExitStack() as held:
        def sb(name, shape, dt):
            return held.enter_context(nc.sbuf_tensor(name, shape, dt))

        m.ident = sb("ident", [P, P], F32)
        m.ident_bf = sb("ident_bf", [P, P], BF16)
        m.mask_qk = sb("mask_qk", [P, P], BF16)
        m.mask_kq = sb("mask_kq", [P, P], BF16)
        m.ones = sb("ones", [P, DH], F32)
        m.slot = sb("slot", [P, NT], I32)
        m.gate = sb("gate", [P, NT], F32)
        m.tile_expert = sb("tile_expert", [1, SLOT_TILES + 1], I32)
        m.alibi_bias = sb("alibi_bias", [P, G * HG * QT], F32)
        m.max_shift = sb("max_shift", [P, G * HG * QT], F32)
        with ExitStack() as c:
            m.w_hi = c.enter_context(nc.sbuf_tensor("w_hi", [P, KC, 3 * D], F32R))
            m.w_lo = c.enter_context(nc.sbuf_tensor("w_lo", [P, KC, 3 * D], F32R))
            m.wg_parts = c.enter_context(nc.sbuf_tensor("wg_parts", [P, KC, P], F32R))
            m.logT = c.enter_context(nc.sbuf_tensor("logT", [2 * E, N], F32))
            make_constants(nc, m)
            project(nc, m)
            route(nc, m)
        attend(nc, m)
        run_experts(nc, m)
        combine(nc, m)


def make_constants(nc, m):
    with ExitStack() as c:
        sb = lambda n, s, d: c.enter_context(nc.sbuf_tensor(n, s, d))
        sem = lambda n: c.enter_context(nc.semaphore(n))
        w_f = sb("w_f", [P, KC, 3 * D], F32)
        wg_f = sb("wg_f", [P, KC, E], F32)
        slopes_row = sb("slopes_row", [1, H], F32)
        slope_col = sb("slope_col", [H, 1], F32)
        key_i = sb("key_i", [H, S], I32)
        key_f = sb("key_f", [H, S], F32)
        sk_hi = sb("sk_hi", [H, S], F32R)
        sk_lo = sb("sk_lo", [H, S], F32R)
        one_f = sb("one_f", [H, S], F32)
        zero_f = sb("zero_f", [P, S], F32)
        rel_i = sb("rel_i", [P, QT], I32)
        rel_f = sb("rel_f", [P, QT], F32)
        first_i = sb("first_i", [P, QT], I32)
        first_f = sb("first_f", [P, QT], F32)

        w_loaded, wg_loaded, slope_loaded = sem("w_loaded"), sem("wg_loaded"), sem("slope_loaded")
        w_hi_done, wg_done = sem("w_hi_done"), sem("wg_done")
        slopes_set, iotas_done, floats_done, filled = (
            sem("slopes_set"), sem("iotas_done"), sem("floats_done"), sem("filled"))
        blank, sk_done, rows_stored, zeros_stored = sem("blank"), sem("sk_done"), sem("rows_stored"), sem("zeros_stored")

        with nc.Block() as block:
            @block.sync
            def _(sp):
                sp.dma_start(w_f[:], m.w_qkv.rearrange("(k p) n -> p k n", p=P)).then_inc(w_loaded, 16)
                sp.dma_start(wg_f[:], m.w_g.rearrange("(k p) n -> p k n", p=P)).then_inc(wg_loaded, 16)
                sp.wait_ge(slopes_set, 1)
                sp.dma_start(slope_col[:, 0:1], slopes_row[0:1, :]).then_inc(slope_loaded, 16)
                sp.wait_ge(filled, 2)
                for r in (2, 3):
                    sp.dma_start(m.k_rows_d[r], one_f[:]).then_inc(rows_stored, 16)
                for r in (0, 1):
                    sp.dma_start(m.q_rows_d[r], one_f[0:HG, :]).then_inc(rows_stored, 16)
                for r in (2, 3, 4, 5):
                    sp.dma_start(m.q_rows_d[r], zero_f[0:HG, :]).then_inc(rows_stored, 16)
                slots = m.slot_x_d.rearrange("(n p) d -> p n d", p=P)
                for n in range(0, SLOTS // P, KC):
                    k = min(KC, SLOTS // P - n)
                    sp.dma_start(slots[:, n:n + k, :], zero_f[:, 0:k * D].rearrange("p (n d) -> p n d", d=D)).then_inc(
                        zeros_stored, 16)
                sp.wait_ge(sk_done, 2)
                sp.dma_start(m.k_rows_d[0], sk_hi[:].bitcast(F32)).then_inc(rows_stored, 16)
                sp.dma_start(m.k_rows_d[1], sk_lo[:].bitcast(F32)).then_inc(rows_stored, 16)
                sp.wait_ge(zeros_stored, 16 * len(range(0, SLOTS // P, KC)))
                sp.wait_ge(rows_stored, 16 * 10)

            @block.gpsimd
            def _(pool):
                for h in range(H):
                    last = nc.gpsimd.memset(slopes_row[0:1, h:h + 1], SLOPES[h])
                last.then_inc(slopes_set, 1)
                nc.gpsimd.iota(key_i[:], [[1, S]], base=0, channel_multiplier=0).then_inc(iotas_done, 1)
                nc.gpsimd.iota(rel_i[:], [[P, QT]], base=-P * (QT - TPC), channel_multiplier=1).then_inc(iotas_done, 1)
                nc.gpsimd.iota(first_i[:], [[CH, QC], [0, TPC]], base=0, channel_multiplier=0).then_inc(iotas_done, 1)
                nc.gpsimd.memset(one_f[:], 1.0).then_inc(filled, 1)
                nc.gpsimd.memset(m.ones[:], 1.0)
                for t in (m.ident, m.ident_bf, m.mask_qk, m.mask_kq):
                    nc.gpsimd.memset(t[:], 0.0).then_inc(blank, 1)
                pool.wait_ge(blank, 4)
                for t in (m.ident, m.ident_bf):
                    nc.gpsimd.affine_select(out=t[:], in_=t[:], compare_op=ALU.not_equal, fill=1.0, base=0,
                                            pattern=[[-1, P]], channel_multiplier=1)
                nc.gpsimd.affine_select(out=m.mask_qk[:], in_=m.mask_qk[:], compare_op=ALU.is_ge, fill=NEG, base=0,
                                        pattern=[[-1, P]], channel_multiplier=1)
                nc.gpsimd.affine_select(out=m.mask_kq[:], in_=m.mask_kq[:], compare_op=ALU.is_ge, fill=NEG, base=0,
                                        pattern=[[1, P]], channel_multiplier=-1)

            @block.scalar
            def _(act):
                act.wait_ge(w_loaded, 16)
                nc.scalar.activation(m.w_hi[:], w_f[:], ACT.Copy).then_inc(w_hi_done, 1)

            @block.vector
            def _(dve):
                nc.vector.memset(zero_f[:], 0.0).then_inc(filled, 1)
                nc.vector.memset(m.wg_parts[:].bitcast(F32), 0.0).then_inc(wg_done, 1)
                dve.wait_ge(wg_loaded, 16)
                dve.wait_ge(wg_done, 1)
                nc.vector.tensor_copy(m.wg_parts[:, :, 0:E], wg_f[:]).then_inc(wg_done, 1)
                dve.wait_ge(wg_done, 2)
                nc.vector.tensor_tensor(m.wg_parts[:, :, E:2 * E], wg_f[:], m.wg_parts[:, :, 0:E].bitcast(F32),
                                        ALU.subtract)
                dve.wait_ge(iotas_done, 3)
                nc.vector.tensor_copy(key_f[:], key_i[:]).then_inc(floats_done, 1)
                nc.vector.tensor_copy(rel_f[:], rel_i[:]).then_inc(floats_done, 1)
                nc.vector.tensor_copy(first_f[:], first_i[:]).then_inc(floats_done, 1)
                dve.wait_ge(floats_done, 3)
                dve.wait_ge(slope_loaded, 16)
                nc.vector.tensor_scalar(sk_hi[:], key_f[:], slope_col[:, 0:1], None, ALU.mult).then_inc(sk_done, 1)
                dve.wait_ge(sk_done, 1)
                nc.vector.scalar_tensor_tensor(sk_lo[:], key_f[:], slope_col[:, 0:1], sk_hi[:].bitcast(F32),
                                               ALU.mult, ALU.subtract).then_inc(sk_done, 1)
                for g in range(G):
                    for hh in range(HG):
                        slope = SLOPES[(g % GB) * HG + hh]
                        o = (g * HG + hh) * QT
                        nc.vector.tensor_scalar(m.alibi_bias[:, o:o + QT], rel_f[:], slope, None, ALU.mult)
                        nc.vector.tensor_scalar(m.max_shift[:, o:o + QT], first_f[:], slope, None, ALU.mult)
                dve.wait_ge(w_hi_done, 1)
                nc.vector.tensor_tensor(m.w_lo[:], w_f[:], m.w_hi[:].bitcast(F32), ALU.subtract)


def project(nc, m):
    NQK = 2 * D // P
    NG = NQK + TPC
    BANKS = 4
    AHEAD = 6
    NV = 12
    with ExitStack() as c:
        sb = lambda n, s, d: c.enter_context(nc.sbuf_tensor(n, s, d))
        pb = lambda n, s, d: c.enter_context(nc.psum_tensor(n, s, d))
        sem = lambda n: c.enter_context(nc.semaphore(n))
        xt = sb("xt", [P, 2, TPC, D], F32)
        xn = sb("xn", [P, 2, TPC, D], F32)
        xT_hi = sb("xT_hi", [P, 2, KC, CH], F32R)
        xT_lo = sb("xT_lo", [P, 2, KC, CH], F32R)
        st_hi = sb("st_hi", [P, BANKS, CH], F32R)
        st_lo = sb("st_lo", [P, BANKS, CH], F32R)
        st_v = sb("st_v", [P, 2, D], F32)
        stats = sb("stats", [P, TPC, 6], F32)
        mean2 = sb("mean2", [P, TPC], F32)
        diff = sb("diff", [P, TPC], F32)
        spread = sb("spread", [P, TPC], F32)
        mean = sb("mean", [P, TPC], F32)
        diff_sq = sb("diff_sq", [P, TPC], F32)
        between = sb("between", [P, TPC], F32)
        var_eps = sb("var_eps", [P, TPC], F32)
        root = sb("root", [P, TPC], F32)
        inv = sb("inv", [P, TPC], F32)
        inv_sq = sb("inv_sq", [P, TPC], F32)
        near_one = sb("near_one", [P, TPC], F32)
        factor = sb("factor", [P, TPC], F32)
        rstd = sb("rstd", [P, TPC], F32)
        group_ps = pb("group_ps", [P, BANKS, CH], F32)
        trans_ps = pb("trans_ps", [P, 2, CH], F32)
        router_ps = pb("router_ps", [P, CH], F32)

        x_loaded = [sem("x_loaded0"), sem("x_loaded1")]
        stats_done, var_done, root_done, xn_done = sem("stats_done"), sem("var_done"), sem("root_done"), sem("xn_done")
        xn_stored = [sem("xn_stored0"), sem("xn_stored1")]
        transposed, tr_hi_done, tr_lo_done = sem("transposed"), sem("tr_hi_done"), sem("tr_lo_done")
        router_done, router_copied = sem("router_done"), sem("router_copied")
        group_done, copied, lo_done = sem("group_done"), sem("copied"), sem("lo_done")
        hi_stored = [sem(f"hi_stored{i}") for i in range(BANKS)]
        lo_stored = [sem(f"lo_stored{i}") for i in range(BANKS)]
        v_stored = [sem("v_stored0"), sem("v_stored1")]

        def chunk_pairs(eng, body):
            body(0, 0, True)
            body(0, 1, True)
            with eng.Fori(1, NCH // 2 - 1) as i:
                body(i, 0, True)
                body(i, 1, True)
            body(NCH // 2 - 1, 0, True)
            body(NCH // 2 - 1, 1, False)

        with nc.Block() as block:
            @block.sync
            def _(sp):
                x_c = m.x.rearrange("(c a p) d -> c p a d", a=TPC, p=P)
                xn_c = m.xn_d.rearrange("(c a p) d -> c p a d", a=TPC, p=P)
                v_c = m.v_d.rearrange("(n p) d -> n p d", p=P)
                sp.dma_start(xt[:, 0], x_c[0]).then_inc(x_loaded[0], 16)
                sp.dma_start(xt[:, 1], x_c[1]).then_inc(x_loaded[1], 16)

                def body(i, half, more):
                    ch = 2 * i + half
                    batch, cc = i // (QC // 2), (i % (QC // 2)) * 2 + half
                    sp.wait_ge(xn_done, (ch + 1) * TPC)
                    sp.dma_start(xn_c[ch], xn[:, half]).then_inc(xn_stored[half], 16)
                    if not isinstance(i, int) or i < NCH // 2 - 1:
                        sp.dma_start(xt[:, half], x_c[ch + 2]).then_inc(x_loaded[half], 16)
                    for e in range(NQK):
                        hi_d, lo_d = (m.q_hi_d, m.q_lo_d) if e < NQK // 2 else (m.k_hi_d, m.k_lo_d)
                        g = batch * GB + e % GB
                        sp.wait_ge(copied, ch * NG + e + 1)
                        sp.dma_start(hi_d[g, :, bass.ts(cc, CH)], st_hi[:, e % BANKS].bitcast(F32)).then_inc(hi_stored[e % BANKS], 16)
                        sp.wait_ge(lo_done, ch * NQK + e + 1)
                        sp.dma_start(lo_d[g, :, bass.ts(cc, CH)], st_lo[:, e % BANKS].bitcast(F32)).then_inc(lo_stored[e % BANKS], 16)
                    for a in range(TPC):
                        sp.wait_ge(copied, ch * NG + NQK + a + 1)
                        sp.dma_start(v_c[ch * TPC + a], st_v[:, a % 2]).then_inc(v_stored[a % 2], 16)

                chunk_pairs(sp, body)
                for s in (*hi_stored, *lo_stored):
                    sp.wait_ge(s, 16 * NCH * NQK // BANKS)
                for s in v_stored:
                    sp.wait_ge(s, 16 * NCH * TPC // 2)
                for s in xn_stored:
                    sp.wait_ge(s, 16 * NCH // 2)

            @block.vector
            def _(dve):
                def norm(ch, i, half):
                    dve.wait_ge(x_loaded[half], 16 * (i + 1))
                    for a in range(TPC):
                        nc.vector.bn_stats(stats[:, a], xt[:, half, a]).then_inc(stats_done, 1)
                    v = ch * NV
                    dve.wait_ge(stats_done, (ch + 1) * TPC)
                    nc.vector.tensor_tensor(mean2[:], stats[:, :, 1], stats[:, :, 4], ALU.add).then_inc(var_done, 1)
                    nc.vector.tensor_tensor(diff[:], stats[:, :, 1], stats[:, :, 4], ALU.subtract).then_inc(var_done, 1)
                    nc.vector.tensor_tensor(spread[:], stats[:, :, 2], stats[:, :, 5], ALU.add).then_inc(var_done, 1)
                    dve.wait_ge(var_done, v + 3)
                    nc.vector.tensor_scalar(mean[:], mean2[:], 0.5, None, ALU.mult).then_inc(var_done, 1)
                    nc.vector.tensor_tensor(diff_sq[:], diff[:], diff[:], ALU.mult).then_inc(var_done, 1)
                    dve.wait_ge(var_done, v + 5)
                    nc.vector.tensor_scalar(between[:], diff_sq[:], 0.25, EPS, ALU.mult, ALU.add).then_inc(var_done, 1)
                    dve.wait_ge(var_done, v + 6)
                    nc.vector.scalar_tensor_tensor(var_eps[:], spread[:], 1.0 / D, between[:], ALU.mult,
                                                   ALU.add).then_inc(var_done, 1)
                    dve.wait_ge(root_done, ch + 1)
                    nc.vector.reciprocal(inv[:], root[:]).then_inc(var_done, 1)
                    dve.wait_ge(var_done, v + 8)
                    nc.vector.tensor_tensor(inv_sq[:], inv[:], inv[:], ALU.mult).then_inc(var_done, 1)
                    dve.wait_ge(var_done, v + 9)
                    nc.vector.tensor_tensor(near_one[:], inv_sq[:], var_eps[:], ALU.mult).then_inc(var_done, 1)
                    dve.wait_ge(var_done, v + 10)
                    nc.vector.tensor_scalar(factor[:], near_one[:], -0.5, 1.5, ALU.mult, ALU.add).then_inc(var_done, 1)
                    dve.wait_ge(var_done, v + 11)
                    nc.vector.tensor_tensor(rstd[:], inv[:], factor[:], ALU.mult).then_inc(var_done, 1)
                    dve.wait_ge(var_done, v + 12)
                    wait_past(dve, xn_stored[half], 16 * i)
                    wait_past(dve, transposed, (ch - 1) * KC)
                    for a in range(TPC):
                        nc.vector.tensor_scalar(xn[:, half, a], xt[:, half, a], mean[:, a:a + 1], rstd[:, a:a + 1],
                                                ALU.subtract, ALU.mult).then_inc(xn_done, 1)

                def low_parts(ch, half):
                    for k in range(KC):
                        dve.wait_ge(tr_hi_done, ch * KC + k + 1)
                        nc.vector.tensor_tensor(xT_lo[:, half, k], trans_ps[:, k % 2], xT_hi[:, half, k].bitcast(F32),
                                                ALU.subtract).then_inc(tr_lo_done, 1)

                def body(i, half, more):
                    ch = 2 * i + half
                    if more:
                        norm(ch + 1, i + half, 1 - half)
                    for e in range(NQK):
                        if e == AHEAD and more:
                            low_parts(ch + 1, 1 - half)
                        dve.wait_ge(copied, ch * NG + e + 1)
                        wait_past(dve, lo_stored[e % BANKS], 16 * (ch * (NQK // BANKS) + e // BANKS))
                        nc.vector.scalar_tensor_tensor(st_lo[:, e % BANKS], group_ps[:, e % BANKS],
                                                       SCALE if e < NQK // 2 else 1.0, st_hi[:, e % BANKS].bitcast(F32),
                                                       ALU.mult, ALU.subtract).then_inc(lo_done, 1)

                norm(0, 0, 0)
                low_parts(0, 0)
                chunk_pairs(dve, body)

            @block.scalar
            def _(act):
                def root_of(ch):
                    act.wait_ge(var_done, ch * NV + 7)
                    nc.scalar.activation(root[:], var_eps[:], ACT.Sqrt).then_inc(root_done, 1)

                def high_parts(ch, half):
                    for k in range(KC):
                        act.wait_ge(transposed, ch * KC + k + 1)
                        nc.scalar.activation(xT_hi[:, half, k], trans_ps[:, k % 2], ACT.Copy).then_inc(tr_hi_done, 1)

                def body(i, half, more):
                    ch = 2 * i + half
                    if more:
                        root_of(ch + 1)
                    act.wait_ge(router_done, ch + 1)
                    nc.scalar.activation(m.logT[:, bass.ts(ch, CH)], router_ps[0:2 * E, :], ACT.Copy).then_inc(
                        router_copied, 1)
                    for e in range(NQK):
                        if e == AHEAD and more:
                            high_parts(ch + 1, 1 - half)
                        act.wait_ge(group_done, ch * NG + e + 1)
                        wait_past(act, hi_stored[e % BANKS], 16 * (ch * (NQK // BANKS) + e // BANKS))
                        nc.scalar.activation(st_hi[:, e % BANKS], group_ps[:, e % BANKS], ACT.Copy,
                                             scale=SCALE if e < NQK // 2 else 1.0).then_inc(copied, 1)
                    for a in range(TPC):
                        act.wait_ge(group_done, ch * NG + NQK + a + 1)
                        wait_past(act, v_stored[a % 2], 16 * (ch * (TPC // 2) + a // 2))
                        nc.scalar.activation(st_v[:, a % 2], group_ps[:, (NQK + a) % BANKS], ACT.Copy).then_inc(copied, 1)

                root_of(0)
                high_parts(0, 0)
                chunk_pairs(act, body)

            @block.tensor
            def _(pe):
                def transposes(ch, half):
                    pe.wait_ge(xn_done, (ch + 1) * TPC)
                    for k in range(KC):
                        wait_past(pe, tr_lo_done, ch * KC + k - 1)
                        for a in range(TPC):
                            last = nc.tensor.transpose(trans_ps[:, k % 2, a * P:(a + 1) * P],
                                                       xn[:, half, a, k * P:(k + 1) * P], m.ident[:])
                        last.then_inc(transposed, 1)

                def body(i, half, more):
                    ch = 2 * i + half
                    pe.wait_ge(tr_lo_done, (ch + 1) * KC)
                    wait_past(pe, router_copied, ch)
                    for k in range(KC):
                        for part in (xT_hi, xT_lo):
                            last = nc.tensor.matmul(router_ps[:], m.wg_parts[:, k], part[:, half, k],
                                                    start=(k == 0 and part is xT_hi), stop=(k == KC - 1 and part is xT_lo))
                    last.then_inc(router_done, 1)
                    for n in range(NG):
                        if n == AHEAD and more:
                            transposes(ch + 1, 1 - half)
                        if n == 0:
                            wait_past(pe, copied, ch * NG)
                        elif n >= BANKS:
                            pe.wait_ge(lo_done, ch * NQK + n - BANKS + 1)
                        for k in range(KC):
                            for p, (x_part, w_part) in enumerate(((xT_hi, m.w_hi), (xT_lo, m.w_hi), (xT_hi, m.w_lo))):
                                if n < NQK:
                                    lhs, rhs = w_part[:, k, n * P:(n + 1) * P], x_part[:, half, k]
                                else:
                                    a = n - NQK
                                    lhs, rhs = x_part[:, half, k, a * P:(a + 1) * P], w_part[:, k, 2 * D:3 * D]
                                last = nc.tensor.matmul(group_ps[:, n % BANKS], lhs, rhs,
                                                        start=(k == 0 and p == 0), stop=(k == KC - 1 and p == 2))
                        last.then_inc(group_done, 1)

                transposes(0, 0)
                chunk_pairs(pe, body)


def route(nc, m):
    with ExitStack() as c:
        sb = lambda n, s, d: c.enter_context(nc.sbuf_tensor(n, s, d))
        pb = lambda n, s, d: c.enter_context(nc.psum_tensor(n, s, d))
        sem = lambda n: c.enter_context(nc.semaphore(n))
        lg = sb("lg", [P, NT, E], F32)
        lg2 = sb("lg2", [P, NT, E], F32)
        ex = sb("ex", [P, NT, E], F32)
        probs = sb("probs", [P, NT, E], F32)
        cand = sb("cand", [P, NT, E], F32)
        hot = sb("hot", [P, NT, E], F32)
        hot_bf = sb("hot_bf", [P, NT, E], BF16)
        totals = sb("totals", [P, NT, E], F32)
        run = [sb("run0", [P, NT, E], F32), sb("run1", [P, NT, E], F32)]
        place = sb("place", [P, NT, E], F32)
        col = sb("col", [P, NT], F32)
        rcp = sb("rcp", [P, NT], F32)
        rank_i = sb("rank_i", [P, E], I32)
        rank_f = sb("rank_f", [P, E], F32)
        full_i = sb("full_i", [P, NT], I32)
        full_f = sb("full_f", [P, NT], F32)
        tile_i = sb("tile_i", [P, SLOT_TILES], I32)
        tile_f = sb("tile_f", [P, SLOT_TILES], F32)
        more = sb("more", [P, E, NT], F32)
        tiles = [sb("tiles0", [P, E], F32), sb("tiles1", [P, E], F32)]
        start = sb("start", [P, E], F32)
        start_row = sb("start_row", [P, E], F32)
        below = sb("below", [P, SLOT_TILES, E], F32)
        expert = sb("expert", [P, SLOT_TILES], F32)
        tri = sb("tri", [P, P], BF16)
        ones_bf = sb("ones_bf", [P, P], BF16)
        log_ps = pb("log_ps", [P, NT, 2 * E], F32)
        rank_ps = pb("rank_ps", [P, NT, E], F32)
        total_ps = pb("total_ps", [P, NT, E], F32)
        logits_ready, exp_done, step_done, hot_ready, counted, made = (
            sem("logits_ready"), sem("exp_done"), sem("step_done"), sem("hot_ready"), sem("counted"), sem("made"))

        with nc.Block() as block:
            @block.gpsimd
            def _(pool):
                nc.gpsimd.memset(tri[:], 1.0).then_inc(made, 1)
                nc.gpsimd.memset(ones_bf[:], 1.0).then_inc(made, 1)
                nc.gpsimd.iota(rank_i[:], [[-1, E]], base=E, channel_multiplier=0).then_inc(made, 1)
                nc.gpsimd.iota(full_i[:], [[P, NT]], base=0, channel_multiplier=0).then_inc(made, 1)
                nc.gpsimd.iota(tile_i[:], [[1, SLOT_TILES]], base=0, channel_multiplier=0).then_inc(made, 1)
                pool.wait_ge(made, 5)
                nc.gpsimd.affine_select(out=tri[:], in_=tri[:], compare_op=ALU.is_gt, fill=0.0, base=0,
                                        pattern=[[1, P]], channel_multiplier=-1).then_inc(made, 1)

            @block.tensor
            def _(pe):
                for n in range(NT):
                    last = nc.tensor.transpose(log_ps[:, n], m.logT[:, n * P:(n + 1) * P], m.ident[0:2 * E, 0:2 * E])
                last.then_inc(logits_ready, 1)
                pe.wait_ge(made, 6)
                pe.wait_ge(hot_ready, 1)
                nc.tensor.matmul(rank_ps[:], tri[:], hot_bf[:], start=True, stop=True)
                nc.tensor.matmul(total_ps[:], ones_bf[:], hot_bf[:], start=True, stop=True).then_inc(counted, 1)

            @block.scalar
            def _(act):
                act.wait_ge(step_done, 6)
                nc.scalar.activation(ex[:], lg[:], ACT.Exp).then_inc(exp_done, 1)

            @block.vector
            def _(dve):
                steps = [0]

                def step(ins):
                    steps[0] += 1
                    ins.then_inc(step_done, 1)
                    dve.wait_ge(step_done, steps[0])

                def by_tile(a):
                    return a.unsqueeze(2).to_broadcast([P, NT, E])

                v = nc.vector
                dve.wait_ge(made, 6)
                step(v.tensor_copy(rank_f[:], rank_i[:]))
                step(v.tensor_copy(full_f[:], full_i[:]))
                dve.wait_ge(logits_ready, 1)
                step(v.tensor_copy(lg2[:], log_ps[:, :, E:2 * E]))
                step(v.tensor_tensor(lg[:], log_ps[:, :, 0:E], lg2[:], ALU.add))
                step(v.tensor_reduce(col[:], lg[:], AX.X, ALU.max))
                step(v.tensor_tensor(lg[:], lg[:], by_tile(col[:]), ALU.subtract))
                dve.wait_ge(exp_done, 1)
                step(v.tensor_reduce(col[:], ex[:], AX.X, ALU.add))
                step(v.reciprocal(rcp[:], col[:]))
                step(v.tensor_tensor(probs[:], ex[:], by_tile(rcp[:]), ALU.mult))
                step(v.tensor_reduce(m.gate[:], probs[:], AX.X, ALU.max))
                step(v.tensor_tensor(cand[:], probs[:], by_tile(m.gate[:]), ALU.is_equal))
                step(v.tensor_tensor(cand[:], cand[:], rank_f[:].unsqueeze(1).to_broadcast([P, NT, E]), ALU.mult))
                step(v.tensor_reduce(col[:], cand[:], AX.X, ALU.max))
                step(v.tensor_tensor(hot[:], cand[:], by_tile(col[:]), ALU.is_equal))
                v.tensor_copy(hot_bf[:], hot[:]).then_inc(hot_ready, 1)
                dve.wait_ge(counted, 1)
                step(v.tensor_copy(totals[:], total_ps[:]))
                step(v.tensor_copy(run[0][:], totals[:]))
                a, b, d = 0, 1, 1
                while d < NT:
                    step(v.tensor_copy(run[b][:, 0:d], run[a][:, 0:d]))
                    step(v.tensor_tensor(run[b][:, d:NT], run[a][:, d:NT], run[a][:, 0:NT - d], ALU.add))
                    a, b, d = b, a, 2 * d
                counts = run[a][:, NT - 1]
                step(v.tensor_tensor(more[:], counts.unsqueeze(2).to_broadcast([P, E, NT]),
                                     full_f[:].unsqueeze(1).to_broadcast([P, E, NT]), ALU.is_gt))
                step(v.tensor_reduce(tiles[0][:], more[:], AX.X, ALU.add))
                step(v.tensor_copy(start[:], tiles[0][:]))
                ta, tb, d = 0, 1, 1
                while d < E:
                    step(v.tensor_copy(tiles[tb][:, 0:d], tiles[ta][:, 0:d]))
                    step(v.tensor_tensor(tiles[tb][:, d:E], tiles[ta][:, d:E], tiles[ta][:, 0:E - d], ALU.add))
                    ta, tb, d = tb, ta, 2 * d
                step(v.tensor_tensor(start[:], tiles[ta][:], start[:], ALU.subtract))
                step(v.tensor_scalar(start_row[:], start[:], float(P), None, ALU.mult))
                step(v.tensor_tensor(place[:], run[a][:], totals[:], ALU.subtract))
                step(v.tensor_tensor(place[:], rank_ps[:], place[:], ALU.add))
                step(v.tensor_tensor(place[:], place[:], start_row[:].unsqueeze(1).to_broadcast([P, NT, E]), ALU.add))
                step(v.tensor_tensor(place[:], place[:], hot[:], ALU.mult))
                step(v.tensor_reduce(col[:], place[:], AX.X, ALU.add))
                step(v.tensor_copy(m.slot[:], col[:]))
                step(v.tensor_copy(tile_f[:], tile_i[:]))
                step(v.tensor_tensor(below[:], start[:].unsqueeze(1).to_broadcast([P, SLOT_TILES, E]),
                                     tile_f[:].unsqueeze(2).to_broadcast([P, SLOT_TILES, E]), ALU.is_le))
                step(v.tensor_reduce(expert[:], below[:], AX.X, ALU.add))
                step(v.tensor_scalar(expert[:], expert[:], -1.0, None, ALU.add))
                step(v.tensor_copy(m.tile_expert[0:1, 0:SLOT_TILES], expert[0:1, :]))


def attend(nc, m):
    with ExitStack() as c:
        sb = lambda n, s, d: c.enter_context(nc.sbuf_tensor(n, s, d))
        pb = lambda n, s, d: c.enter_context(nc.psum_tensor(n, s, d))
        sem = lambda n: c.enter_context(nc.semaphore(n))
        q_aug = sb("q_aug", [P, 2, HG, S], F32R)
        k_aug = sb("k_aug", [P, 2, HG, S], F32R)
        v_sb = sb("v_sb", [P, 2, QT, P], F32)
        probs = sb("probs_sb", [P, P_SLOTS, HG, CH], F32)
        pair_sum = sb("pair_sum", [P, 2, HG, CH], F32)
        bias = sb("bias", [P, 2, HG * QT], F32)
        part_max = sb("part_max", [P, QT * HG, QC], F32)
        row_max = sb("row_max", [P, HG * QT], F32)
        neg_max = sb("neg_max", [P, P], F32)
        max_hi = sb("max_hi", [HG * QT, P], F32R)
        max_lo = sb("max_lo", [HG * QT, P], F32R)
        inv_den = sb("inv_den", [P, CH], F32)
        y_sb = sb("y_sb", [P, 2, CH], F32)
        score_ps = pb("score_ps", [P, S_BANKS, CH], F32)
        max_ps = pb("max_ps", [P, M_BANKS, CH], F32)
        y_ps = pb("y_ps", [P, CH], F32)
        den_ps = pb("den_ps", [P, CH], F32)

        aug_loaded = [sem("aug_loaded0"), sem("aug_loaded1")]
        v_loaded = [sem("v_loaded0"), sem("v_loaded1")]
        max_rows_loaded, y_stored = sem("max_rows_loaded"), [sem("y_stored0"), sem("y_stored1")]
        max_scored, max_taken = sem("max_scored"), sem("max_taken")
        max_blank, folded, neg_done, max_turned, max_hi_done, max_lo_done = (
            sem("max_blank"), sem("folded"), sem("neg_done"), sem("max_turned"), sem("max_hi_done"), sem("max_lo_done"))
        bias_ready, scored, exp_done, pv_done, pair_added, pair_used = (
            sem("bias_ready"), sem("scored"), sem("probs_ready"), sem("pv_done"), sem("pair_added"), sem("pair_used"))
        inv_done, y_done = sem("inv_done"), sem("y_done")
        xn_loaded, slots_stored = sem("xn_loaded"), sem("slots_stored")
        AUG = 16 * 8

        def groups(eng, step):
            step(0, 0, True, False)
            step(1, 1, False, False)
            with eng.Fori(1, G // 2 - 1) as i:
                step(2 * i, 0, False, False)
                step(2 * i + 1, 1, False, False)
            step(G - 2, 0, False, False)
            step(G - 1, 1, False, True)

        def base(eng, g, per_group):
            if isinstance(g, int):
                return g * per_group
            r = eng.alloc_register(f"base{nc.next_id()}")
            eng.reg_mov(r, g * per_group)
            return eng.snap(r, min_val=2 * per_group, max_val=G * per_group)

        with nc.Block() as block:
            @block.sync
            def _(sp):
                def load(g, half):
                    wait_past(sp, pv_done, (g - 1) * NR)
                    for part, (kk, qq) in enumerate(((m.k_hi_d, m.q_hi_d), (m.k_lo_d, m.q_hi_d), (m.k_hi_d, m.q_lo_d))):
                        rows = slice(part * DH, (part + 1) * DH)
                        sp.dma_start(k_aug[rows, half].bitcast(F32), kk[g].rearrange("(h d) n -> d h n", d=DH)).then_inc(aug_loaded[half], 16)
                        sp.dma_start(q_aug[rows, half].bitcast(F32), qq[g].rearrange("(h d) n -> d h n", d=DH)).then_inc(aug_loaded[half], 16)
                    gb = g % GB
                    sp.dma_start(k_aug[ROW_ALIBI:ROWS, half].bitcast(F32), m.k_rows_d.rearrange("r (g h) n -> g r h n", h=HG)[gb]).then_inc(
                        aug_loaded[half], 16)
                    sp.dma_start(q_aug[ROW_ALIBI:ROWS, half].bitcast(F32), m.q_rows_d[0:4]).then_inc(aug_loaded[half], 16)
                    v_bg = m.v_d.rearrange("(b j p) (g e) -> b g p j e", b=B, p=P, e=P)
                    sp.dma_start(v_sb[:, half], v_bg[g // GB, gb]).then_inc(v_loaded[half], 16)

                def max_rows(g, half):
                    sp.wait_ge(max_hi_done, g + 1)
                    sp.wait_ge(max_lo_done, g + 1)
                    sp.dma_start(q_aug[ROW_ALIBI:ROW_MAX, half].bitcast(F32), m.q_rows_d[4:6]).then_inc(max_rows_loaded, 16)
                    sp.dma_start(q_aug[ROW_MAX:ROW_MAX + 1, half].bitcast(F32), max_hi[:].bitcast(F32)).then_inc(max_rows_loaded, 16)
                    sp.dma_start(q_aug[ROW_MAX + 1:ROWS, half].bitcast(F32), max_lo[:].bitcast(F32)).then_inc(max_rows_loaded, 16)

                def step(g, half, first, last):
                    if not last:
                        load(g + 1, 1 - half)
                    for cc in range(QC):
                        if cc == QC - 1 and not last:
                            max_rows(g + 1, 1 - half)
                        sp.wait_ge(y_done, g * QC + cc + 1)
                        sp.dma_start(m.y_d[g, :, cc * CH:(cc + 1) * CH], y_sb[:, cc % 2]).then_inc(y_stored[cc % 2], 16)

                load(0, 0)
                max_rows(0, 0)
                groups(sp, step)
                for s in y_stored:
                    sp.wait_ge(s, 16 * G * QC // 2)

            @block.gpsimd
            def _(pool):
                rows_sb = probs[:].rearrange("p s h n -> p (s h) n")
                xn_t = m.xn_d.rearrange("(n p) d -> p n d", p=P)
                turn = P_SLOTS * HG
                for k in range(NT // turn):
                    if k:
                        pool.wait_ge(slots_stored, 16 * turn * k)
                    pool.dma_start(rows_sb, xn_t[:, k * turn:(k + 1) * turn]).then_inc(xn_loaded, 16)
                    pool.wait_ge(xn_loaded, 16 * (k + 1))
                    for n in range(turn):
                        pool.indirect_dma_start(
                            m.slot_x_d, bass.IndirectOffsetOnAxis(ap=m.slot[:, k * turn + n:k * turn + n + 1], axis=0),
                            rows_sb[:, n], None).then_inc(slots_stored, 16)

                def bias_of(g, half):
                    wait_past(pool, exp_done, (g - 1) * NSU)
                    nc.gpsimd.tensor_copy(bias[:, half], m.alibi_bias[:, bass.ts(g, HG * QT)]).then_inc(bias_ready, 1)

                bias_of(0, 0)
                pool.wait_ge(slots_stored, 16 * NT)

                def step(g, half, first, last):
                    if not last:
                        bias_of(g + 1, 1 - half)
                    exps, used = base(pool, g, NSU), base(pool, g, NPAIR)
                    for p in range(NPAIR):
                        r1 = PAIR_LAST[p]
                        s0, s1 = (r1 - 1) % P_SLOTS, r1 % P_SLOTS
                        if not (first and p < 2):
                            pool.wait_ge(pair_used, used + (p - 1))
                        for hh in range(HG):
                            pool.wait_ge(exp_done, exps + (r1 * HG + hh + 1))
                            nc.gpsimd.tensor_tensor(pair_sum[:, p % 2, hh], probs[:, s0, hh], probs[:, s1, hh],
                                                    ALU.add).then_inc(pair_added, 1)

                groups(pool, step)

            @block.vector
            def _(dve):
                nc.vector.memset(part_max[:], -3.0e38).then_inc(max_blank, 1)
                nc.vector.memset(neg_max[:], 0.0).then_inc(max_blank, 1)
                dve.wait_ge(max_blank, 2)

                def take_max(u, units):
                    i, kc, hh = MAX_UNITS[u]
                    w = min(CH, (i + 1) * P - kc * CH)
                    dve.wait_ge(max_scored, units + (u + 1))
                    nc.vector.tensor_reduce(part_max[:, hh * QT + i, kc:kc + 1], max_ps[:, u % M_BANKS, 0:w], AX.X,
                                            ALU.max).then_inc(max_taken, 1)

                def fold(g):
                    dve.wait_ge(max_taken, (g + 1) * NMU)
                    nc.vector.tensor_reduce(row_max[:], part_max[:], AX.X, ALU.max).then_inc(folded, 1)
                    dve.wait_ge(folded, g + 1)
                    nc.vector.tensor_tensor(neg_max[:, 0:HG * QT], m.max_shift[:, bass.ts(g, HG * QT)], row_max[:],
                                            ALU.subtract).then_inc(neg_done, 1)

                def low_row(g):
                    dve.wait_ge(max_hi_done, g + 1)
                    nc.vector.tensor_tensor(max_lo[:], max_ps[0:HG * QT, 0, 0:P], max_hi[:].bitcast(F32),
                                            ALU.subtract).then_inc(max_lo_done, 1)

                def finish(g, cc):
                    n = g * QC + cc
                    dve.wait_ge(pv_done, g * NR + LAST_ROUND[cc] + 1)
                    nc.vector.reciprocal(inv_den[:], den_ps[:]).then_inc(inv_done, 1)
                    dve.wait_ge(inv_done, n + 1)
                    wait_past(dve, y_stored[cc % 2], 16 * (g * (QC // 2) + cc // 2))
                    nc.vector.tensor_tensor(y_sb[:, cc % 2], y_ps[:], inv_den[:], ALU.mult).then_inc(y_done, 1)

                def step(g, half, first, last):
                    units = None if last else base(dve, g + 1, NMU)
                    for r in range(NR + 1):
                        if not last:
                            for u in max_units_of(r):
                                take_max(u, units)
                            if r == FOLD_AT:
                                fold(g + 1)
                            if r == FOLD_AT + 1:
                                low_row(g + 1)
                        if r - 1 in LAST_ROUND:
                            finish(g, LAST_ROUND.index(r - 1))

                for u in range(NMU):
                    take_max(u, 0)
                fold(0)
                low_row(0)
                groups(dve, step)

            @block.scalar
            def _(act):
                def high_row(g):
                    act.wait_ge(max_turned, g + 1)
                    nc.scalar.activation(max_hi[:], max_ps[0:HG * QT, 0, 0:P], ACT.Copy).then_inc(max_hi_done, 1)

                def step(g, half, first, last):
                    act.wait_ge(bias_ready, g + 1)
                    units, rounds, adds = base(act, g, NSU), base(act, g, NR), base(act, g, NPAIR * HG)
                    for r, (cc, jb) in enumerate(ROUNDS):
                        off = max(0, jb - TPC * cc) * P
                        back, e = earlier_user(r, P_SLOTS, NR)
                        if not (first and back):
                            act.wait_ge(pv_done, rounds + (e + 1 - back * NR))
                            if e in PAIR_OF:
                                act.wait_ge(pair_added, adds + ((PAIR_OF[e] + 1 - back * NPAIR) * HG))
                        elif r == 0:
                            act.wait_ge(slots_stored, 16 * NT)
                        dist = jb - TPC * cc + QT - TPC
                        for hh in range(HG):
                            act.wait_ge(scored, units + (r * HG + hh + 1))
                            nc.scalar.activation(probs[:, r % P_SLOTS, hh, off:CH],
                                                 score_ps[:, (r * HG + hh) % S_BANKS, off:CH], ACT.Exp,
                                                 bias=bias[:, half, hh * QT + dist:hh * QT + dist + 1]).then_inc(exp_done, 1)
                        if r == FOLD_AT and not last:
                            high_row(g + 1)

                high_row(0)
                groups(act, step)

            @block.tensor
            def _(pe):
                def max_unit(half, u, taken):
                    i, kc, hh = MAX_UNITS[u]
                    w = min(CH, (i + 1) * P - kc * CH)
                    diag = kc == i // TPC
                    bank = u % M_BANKS
                    back, e = earlier_user(u, M_BANKS, NMU)
                    if not (back and isinstance(taken, int) and taken == 0):
                        pe.wait_ge(max_taken, taken + (e + 1 - back * NMU))
                    last = nc.tensor.matmul(max_ps[:, bank, 0:w], q_aug[0:ROW_MAX, half, hh, i * P:(i + 1) * P],
                                            k_aug[0:ROW_MAX, half, hh, kc * CH:kc * CH + w], start=True, stop=not diag)
                    if diag:
                        last = nc.tensor.matmul(max_ps[:, bank, w - P:w], m.ident_bf[:], m.mask_qk[:], start=False, stop=True)
                    last.then_inc(max_scored, 1)

                def turn_max(g):
                    pe.wait_ge(neg_done, g + 1)
                    nc.tensor.transpose(max_ps[:, 0, 0:P], neg_max[:], m.ident[:]).then_inc(max_turned, 1)

                def score_unit(half, r, hh, first, exps):
                    cc, jb = ROUNDS[r]
                    off = max(0, jb - TPC * cc) * P
                    diag = jb >= TPC * cc
                    u = r * HG + hh
                    back, e = earlier_user(u, S_BANKS, NSU)
                    if not (first and back):
                        pe.wait_ge(exp_done, exps + (e + 1 - back * NSU))
                    last = nc.tensor.matmul(score_ps[:, u % S_BANKS, off:CH], k_aug[0:ROWS, half, hh, jb * P:(jb + 1) * P],
                                            q_aug[0:ROWS, half, hh, cc * CH + off:(cc + 1) * CH], start=True, stop=not diag)
                    if diag:
                        last = nc.tensor.matmul(score_ps[:, u % S_BANKS, off:off + P], m.ident_bf[:], m.mask_kq[:],
                                                start=False, stop=True)
                    last.then_inc(scored, 1)

                def pair_product(p, start, adds):
                    for hh in range(HG):
                        pe.wait_ge(pair_added, adds + (p * HG + hh + 1))
                        last = nc.tensor.matmul(den_ps[hh * DH:(hh + 1) * DH, :], m.ones[:], pair_sum[:, p % 2, hh],
                                                start=start, stop=False)
                    last.then_inc(pair_used, 1)

                def value_products(g, half, r, exps, adds):
                    cc, jb = ROUNDS[r]
                    off = max(0, jb - TPC * cc) * P
                    final = r == LAST_ROUND[cc]
                    if jb == 0:
                        wait_past(pe, y_done, g * QC + cc)
                    pe.wait_ge(exp_done, exps + (r + 1) * HG)
                    if r - 2 in PAIR_LAST.values():
                        p = PAIR_OF[r - 2]
                        pair_product(p, ROUNDS[r - 2] == (cc, 1), adds)
                    if r not in PAIR_OF:
                        for hh in range(HG):
                            nc.tensor.matmul(den_ps[hh * DH:(hh + 1) * DH, off:CH], m.ones[:],
                                             probs[:, r % P_SLOTS, hh, off:CH], start=jb == 0, stop=final)
                    for hh in range(HG):
                        last = nc.tensor.matmul(y_ps[hh * DH:(hh + 1) * DH, off:CH],
                                                v_sb[:, half, jb, hh * DH:(hh + 1) * DH],
                                                probs[:, r % P_SLOTS, hh, off:CH], start=jb == 0, stop=final)
                    last.then_inc(pv_done, 1)

                def step(g, half, first, last):
                    pe.wait_ge(max_rows_loaded, 48 * (g + 1))
                    pe.wait_ge(v_loaded[half], 16 * (g // 2 + 1))
                    exps, adds = base(pe, g, NSU), base(pe, g, NPAIR * HG)
                    taken = None if last else base(pe, g + 1, NMU)
                    for r in range(NR + 1):
                        units = [] if last else list(max_units_of(r))
                        if units and units[0] == 0:
                            pe.wait_ge(aug_loaded[1 - half], AUG * ((g + 1) // 2 + 1))
                        for hh in range(HG):
                            if r < NR:
                                score_unit(half, r, hh, first, exps)
                            for u in units[len(units) * hh // HG:len(units) * (hh + 1) // HG]:
                                max_unit(1 - half, u, taken)
                        if r == FOLD_AT and not last:
                            turn_max(g + 1)
                        if r:
                            value_products(g, half, r - 1, exps, adds)

                pe.wait_ge(aug_loaded[0], AUG)
                for u in range(NMU):
                    max_unit(0, u, 0)
                turn_max(0)
                groups(pe, step)


def run_experts(nc, m):
    with ExitStack() as c:
        sb = lambda n, s, d: c.enter_context(nc.sbuf_tensor(n, s, d))
        pb = lambda n, s, d: c.enter_context(nc.psum_tensor(n, s, d))
        sem = lambda n: c.enter_context(nc.semaphore(n))
        w_nat = sb("w_nat", [P, 2, KC, D], F32)
        wT_hi = sb("wT_hi", [P, E, KC, D], F32R)
        wT_lo = sb("wT_lo", [P, E, KC, D], F32R)
        bias_all = sb("bias_all", [P, E, D], F32)
        rows = sb("rows", [P, 2, D], F32)
        rT_hi = sb("rT_hi", [P, 2, KC, P], F32R)
        rT_lo = sb("rT_lo", [P, 2, KC, P], F32R)
        y_rows = sb("y_rows", [P, 2, D], F32)
        turn_ps = pb("turn_ps", [P, 4, D], F32)
        prod_ps = pb("prod_ps", [P, 2, D], F32)

        w_loaded = [sem("we_loaded0"), sem("we_loaded1")]
        b_loaded = sem("b_loaded")
        rows_loaded = [sem("rows_loaded0"), sem("rows_loaded1")]
        turned, hi_done, lo_done = sem("w_turned"), sem("w_hi_done2"), sem("w_lo_done2")
        r_turned, r_hi_done, r_lo_done = sem("r_turned"), sem("r_hi_done"), sem("r_lo_done")
        prod_done, y_done = sem("prod_done"), sem("y_rows_done")
        y_stored = [sem("y_rows_stored0"), sem("y_rows_stored1")]
        NW = E * KC

        def tile_pairs(eng, body):
            body(0, 0, 0, True)
            body(1, 0, 1, True)
            with eng.Fori(1, SLOT_TILES // 2) as i:
                body(2 * i, i, 0, True)
                body(2 * i + 1, i, 1, True)
            body(SLOT_TILES - 1, SLOT_TILES // 2, 0, False)

        with nc.Block() as block:
            x_t = m.slot_x_d.rearrange("(n p) d -> n p d", p=P)
            y_t = m.slot_y_d.rearrange("(n p) d -> n p d", p=P)

            @block.sync
            def _(sp):
                for e in range(E):
                    if e >= 2:
                        sp.wait_ge(turned, (e - 1) * KC)
                    sp.dma_start(w_nat[:, e % 2], m.w_e[e].rearrange("(k p) n -> p k n", p=P)).then_inc(w_loaded[e % 2], 16)
                sp.dma_start(bias_all[:], m.b_e.partition_broadcast(P)).then_inc(b_loaded, 16)
                sp.dma_start(rows[:, 0], x_t[0]).then_inc(rows_loaded[0], 16)
                sp.dma_start(rows[:, 1], x_t[1]).then_inc(rows_loaded[1], 16)

                def body(j, i, half, more):
                    if more:
                        sp.wait_ge(r_turned, j + 1)
                        sp.dma_start(rows[:, half], x_t[j + 2]).then_inc(rows_loaded[half], 16)
                    sp.wait_ge(y_done, j + 1)
                    sp.dma_start(y_t[j], y_rows[:, half]).then_inc(y_stored[half], 16)

                tile_pairs(sp, body)
                sp.wait_ge(rows_loaded[1], 16 * (SLOT_TILES // 2 + 1))
                sp.wait_ge(y_stored[0], 16 * ((SLOT_TILES + 1) // 2))
                sp.wait_ge(y_stored[1], 16 * (SLOT_TILES // 2))

            @block.scalar
            def _(act):
                for u in range(NW):
                    act.wait_ge(turned, u + 1)
                    nc.scalar.activation(wT_hi[:, u // KC, u % KC], turn_ps[:, u % 4], ACT.Copy).then_inc(hi_done, 1)

                def high_part(j, half):
                    act.wait_ge(r_turned, j + 1)
                    wait_past(act, prod_done, j - 1)
                    nc.scalar.activation(rT_hi[:, half], turn_ps[:, half].rearrange("p (k n) -> p k n", n=P),
                                         ACT.Copy).then_inc(r_hi_done, 1)

                def body(j, i, half, more):
                    if more:
                        high_part(j + 1, 1 - half)

                high_part(0, 0)
                tile_pairs(act, body)

            @block.vector
            def _(dve):
                for u in range(NW):
                    dve.wait_ge(hi_done, u + 1)
                    nc.vector.tensor_tensor(wT_lo[:, u // KC, u % KC], turn_ps[:, u % 4],
                                            wT_hi[:, u // KC, u % KC].bitcast(F32), ALU.subtract).then_inc(lo_done, 1)

                def low_part(j, half):
                    dve.wait_ge(r_hi_done, j + 1)
                    nc.vector.tensor_tensor(rT_lo[:, half], turn_ps[:, half].rearrange("p (k n) -> p k n", n=P),
                                            rT_hi[:, half].bitcast(F32), ALU.subtract).then_inc(r_lo_done, 1)

                def body(j, i, half, more):
                    if more:
                        low_part(j + 1, 1 - half)
                    e = dve.value_load(m.tile_expert[0:1, bass.ds(j, 1)], min_val=0, max_val=E - 1)
                    dve.wait_ge(prod_done, j + 1)
                    wait_past(dve, y_stored[half], 16 * i)
                    nc.vector.tensor_tensor(y_rows[:, half], prod_ps[:, half], bias_all[:, e], ALU.add).then_inc(y_done, 1)

                low_part(0, 0)
                dve.wait_ge(b_loaded, 16)
                tile_pairs(dve, body)

            @block.tensor
            def _(pe):
                for u in range(NW):
                    e, k = u // KC, u % KC
                    if k == 0:
                        pe.wait_ge(w_loaded[e % 2], 16 * (e // 2 + 1))
                    if u >= 4:
                        pe.wait_ge(lo_done, u - 3)
                    for a in range(KC):
                        last = nc.tensor.transpose(turn_ps[:, u % 4, a * P:(a + 1) * P],
                                                   w_nat[:, e % 2, a, k * P:(k + 1) * P], m.ident[:])
                    last.then_inc(turned, 1)
                pe.wait_ge(lo_done, NW)

                def turn_rows(j, i, half):
                    pe.wait_ge(rows_loaded[half], 16 * (i + 1))
                    wait_past(pe, r_lo_done, j - 1)
                    for k in range(KC):
                        last = nc.tensor.transpose(turn_ps[:, half, k * P:(k + 1) * P], rows[:, half, k * P:(k + 1) * P],
                                                   m.ident[:])
                    last.then_inc(r_turned, 1)

                def body(j, i, half, more):
                    if more:
                        turn_rows(j + 1, i + half, 1 - half)
                    e = pe.value_load(m.tile_expert[0:1, bass.ds(j, 1)], min_val=0, max_val=E - 1)
                    pe.wait_ge(r_lo_done, j + 1)
                    wait_past(pe, y_done, j - 1)
                    for k in range(KC):
                        for p, (r_part, w_part) in enumerate(((rT_hi, wT_hi), (rT_lo, wT_hi), (rT_hi, wT_lo))):
                            last = nc.tensor.matmul(prod_ps[:, half], r_part[:, half, k], w_part[:, e, k],
                                                    start=(k == 0 and p == 0), stop=(k == KC - 1 and p == 2))
                    last.then_inc(prod_done, 1)

                turn_rows(0, 0, 0)
                tile_pairs(pe, body)


def combine(nc, m):
    with ExitStack() as c:
        sb = lambda n, s, d: c.enter_context(nc.sbuf_tensor(n, s, d))
        pb = lambda n, s, d: c.enter_context(nc.psum_tensor(n, s, d))
        sem = lambda n: c.enter_context(nc.semaphore(n))
        wo_f = sb("wo_f", [P, KC, D], F32)
        wo_hi = sb("wo_hi", [P, KC, D], F32R)
        wo_lo = sb("wo_lo", [P, KC, D], F32R)
        yT = sb("yT", [P, 2, KC, CH], F32)
        yT_hi = sb("yT_hi", [P, 2, KC, CH], F32R)
        yT_lo = sb("yT_lo", [P, 2, KC, CH], F32R)
        x_sb = sb("x_sb", [P, 2, TPC, D], F32)
        e_sb = sb("e_sb", [P, 2, TPC, D], F32)
        r_sb = sb("r_sb", [P, TPC, D], F32)
        o_sb = sb("o_sb", [P, 2, TPC, D], F32)
        attn_ps = pb("attn_ps", [P, 4, D], F32)

        wo_loaded, wo_hi_done, wo_done = sem("wo_loaded"), sem("wo_hi_done"), sem("wo_done")
        yT_loaded = [sem("yT_loaded0"), sem("yT_loaded1")]
        x_loaded = [sem("x2_loaded0"), sem("x2_loaded1")]
        e_loaded = [sem("e_loaded0"), sem("e_loaded1")]
        yT_hi_done, yT_lo_done, attn_done, added, out_done = (
            sem("yT_hi_done"), sem("yT_lo_done"), sem("attn_done"), sem("added"), sem("out_done"))
        out_stored = [sem("out_stored0"), sem("out_stored1")]

        def chunk_pairs(eng, body):
            body(0, 0, 0)
            body(1, 0, 1)
            with eng.Fori(1, NCH // 2 - 1) as i:
                body(2 * i, i, 0)
                body(2 * i + 1, i, 1)
            body(NCH - 2, NCH // 2 - 1, 0)
            body(NCH - 1, NCH // 2 - 1, 1)

        def is_last(ch):
            return isinstance(ch, int) and ch == NCH - 1

        with nc.Block() as block:
            x_c = m.x.rearrange("(c a p) d -> c p a d", a=TPC, p=P)
            o_c = m.out.rearrange("(c a p) d -> c p a d", a=TPC, p=P)
            y_c = m.y_d.rearrange("(b g) p (c n) -> b c p g n", b=B, n=CH)

            @block.sync
            def _(sp):
                def load(ch, i, half):
                    wait_past(sp, added, (ch - 1) * TPC)
                    sp.dma_start(yT[:, half], y_c[ch // QC, ch % QC]).then_inc(yT_loaded[half], 16)
                    sp.dma_start(x_sb[:, half], x_c[ch]).then_inc(x_loaded[half], 16)

                sp.dma_start(wo_f[:], m.w_o.rearrange("(k p) n -> p k n", p=P)).then_inc(wo_loaded, 16)
                load(0, 0, 0)

                def body(ch, i, half):
                    if not is_last(ch):
                        load(ch + 1, i + half, 1 - half)
                    sp.wait_ge(out_done, (ch + 1) * TPC)
                    sp.dma_start(o_c[ch], o_sb[:, half]).then_inc(out_stored[half], 16)

                chunk_pairs(sp, body)
                for s in out_stored:
                    sp.wait_ge(s, 16 * NCH // 2)

            @block.gpsimd
            def _(pool):
                def body(ch, i, half):
                    wait_past(pool, out_done, (ch - 1) * TPC)
                    for a in range(TPC):
                        pool.indirect_dma_start(
                            e_sb[:, half, a], None, m.slot_y_d,
                            bass.IndirectOffsetOnAxis(ap=m.slot[:, bass.ds(ch * TPC + a, 1)], axis=0)).then_inc(
                                e_loaded[half], 16)

                for ch in range(NCH):
                    body(ch, ch // 2, ch % 2)

            @block.scalar
            def _(act):
                act.wait_ge(wo_loaded, 16)
                nc.scalar.activation(wo_hi[:], wo_f[:], ACT.Copy).then_inc(wo_hi_done, 1)

                def body(ch, i, half):
                    act.wait_ge(yT_loaded[half], 16 * (i + 1))
                    wait_past(act, attn_done, (ch - 1) * TPC)
                    nc.scalar.activation(yT_hi[:, half], yT[:, half], ACT.Copy).then_inc(yT_hi_done, 1)

                chunk_pairs(act, body)

            @block.vector
            def _(dve):
                dve.wait_ge(wo_hi_done, 1)
                nc.vector.tensor_tensor(wo_lo[:], wo_f[:], wo_hi[:].bitcast(F32), ALU.subtract).then_inc(wo_done, 1)

                def low_part(ch, half):
                    dve.wait_ge(yT_hi_done, ch + 1)
                    nc.vector.tensor_tensor(yT_lo[:, half], yT[:, half], yT_hi[:, half].bitcast(F32),
                                            ALU.subtract).then_inc(yT_lo_done, 1)

                def body(ch, i, half):
                    for a in range(TPC):
                        if a == 1 and not is_last(ch):
                            low_part(ch + 1, 1 - half)
                        if a == 0:
                            dve.wait_ge(x_loaded[half], 16 * (i + 1))
                            dve.wait_ge(e_loaded[half], 16 * TPC * (i + 1))
                            wait_past(dve, out_stored[half], 16 * i)
                        dve.wait_ge(attn_done, ch * TPC + a + 1)
                        nc.vector.tensor_tensor(r_sb[:, a], attn_ps[:, a], x_sb[:, half, a], ALU.add).then_inc(added, 1)
                        dve.wait_ge(added, ch * TPC + a + 1)
                        nc.vector.scalar_tensor_tensor(o_sb[:, half, a], e_sb[:, half, a],
                                                       m.gate[:, bass.ds(ch * TPC + a, 1)], r_sb[:, a],
                                                       ALU.mult, ALU.add).then_inc(out_done, 1)

                low_part(0, 0)
                chunk_pairs(dve, body)

            @block.tensor
            def _(pe):
                pe.wait_ge(wo_done, 1)

                def body(ch, i, half):
                    pe.wait_ge(yT_lo_done, ch + 1)
                    for a in range(TPC):
                        wait_past(pe, added, (ch - 1) * TPC + a + 1)
                        for k in range(KC):
                            for p, (y_part, w_part) in enumerate(((yT_hi, wo_hi), (yT_lo, wo_hi), (yT_hi, wo_lo))):
                                last = nc.tensor.matmul(attn_ps[:, a], y_part[:, half, k, a * P:(a + 1) * P], w_part[:, k],
                                                        start=(k == 0 and p == 0), stop=(k == KC - 1 and p == 2))
                        last.then_inc(attn_done, 1)

                chunk_pairs(pe, body)


def kernel(**inputs):
    import concourse.bacc as bacc
    from concourse.bass_utils import run_bass_kernel_spmd

    names = ["L0_attn_x", "L0_attn_W_qkv", "L0_attn_W_o", "L0_ffn_wg", "L0_ffn_W", "L0_ffn_b"]
    nc = bacc.Bacc("TRN2", target_bir_lowering=False, num_devices=1)
    arrays, args = {}, []
    for name in names:
        a = np.ascontiguousarray(inputs[name])
        arrays[f"in_{name}"] = a
        args.append(nc.dram_tensor(f"in_{name}", a.shape, mybir.dt.from_np(a.dtype), kind="ExternalInput").ap())
    args.append(nc.dram_tensor("out_rows", (B, S, D), F32, kind="ExternalOutput").ap())
    prenorm_alibi_attention_plus_top1_experts(nc, *args)
    r = run_bass_kernel_spmd(nc, [arrays], core_ids=[0])
    return r.results[0]["out_rows"]
```

```python
from contextlib import ExitStack

import numpy as np

import concourse.bass as bass
from concourse import mybir
from concourse.alu_op_type import AluOpType as ALU

F32 = mybir.dt.float32
F32R = mybir.dt.float32r
BF16 = mybir.dt.bfloat16
I32 = mybir.dt.int32
ACT = mybir.ActivationFunctionType
AX = mybir.AxisListType

P = 128
B, S, D = 2, 2048, 512
H, DH = 16, 32
E = 8
N = B * S
CH = 512
NCH = N // CH
TPC = CH // P
NT = N // P
KC = D // P
HG = P // DH
G = B * H // HG
GB = H // HG
QT = S // P
QC = S // CH
SLOT_TILES = NT + E - 1
SLOTS = (SLOT_TILES + 1) * P
Y_BUFS = 2
EPS = 1e-5
NEG = -1e30
SCALE = float(np.float32(1.0) / np.sqrt(np.float32(DH)))
SLOPES = [float(np.float32(2.0) ** (np.float32(-8.0) / np.float32(i))) for i in range(1, H + 1)]

ROW_ALIBI = 3 * DH
ROW_MAX = ROW_ALIBI + 2
ROWS = ROW_MAX + 2

ROUNDS = [(c, jb) for c in range(QC) for jb in range(TPC * (c + 1))]
NR = len(ROUNDS)
MAX_UNITS = [(i, kc, hh) for i in range(QT) for kc in range(i // TPC + 1) for hh in range(HG)]
NMU = len(MAX_UNITS)
NSU = NR * HG
S_BANKS, M_BANKS, P_SLOTS = 3, 3, 4
PAIR_OF = {}
for _r, (_c, _jb) in enumerate(ROUNDS):
    if _jb < TPC * _c:
        PAIR_OF[_r] = len(PAIR_OF) // 2
NPAIR = len(PAIR_OF) // 2
PAIR_LAST = {p: r for r, p in PAIR_OF.items()}
LAST_ROUND = [max(r for r, (cc, _) in enumerate(ROUNDS) if cc == c) for c in range(QC)]

UNIT, FOLD, TURN, SPLIT = "unit", "fold", "turn", "split"
OF_CHUNK = [[u for u, (i, _, _) in enumerate(MAX_UNITS) if i // TPC == c] for c in range(QC)]


def spread(events, rounds):
    n = len(rounds)
    return {r: events[len(events) * k // n:len(events) * (k + 1) // n] for k, r in enumerate(rounds)}


def units_of(dg, *chunks):
    return [(dg, UNIT, u) for c in chunks for u in OF_CHUNK[c]]


def plan(parts, chains):
    out = [[] for _ in range(NR)]
    for part in parts:
        for r, events in part.items():
            out[r] += events
    for dg, c, r in chains:
        out[r] = [(dg, FOLD, c), *out[r], (dg, TURN, c)]
        out[r + 1] = [(dg, SPLIT, c), *out[r + 1]]
    return out


AHEAD = 14
RATE = NMU // NR
STREAM = units_of(1, *range(QC))
EARLY = STREAM[:RATE * (NR - AHEAD)]
LATE = [(0, UNIT, u) for _, _, u in STREAM[RATE * (NR - AHEAD):]]
PLAN_MID = plan([spread(LATE, range(0, AHEAD)), spread(EARLY, range(AHEAD, NR))],
                [(0, 3, AHEAD), (1, 0, AHEAD + 4), (1, 1, AHEAD + 12), (1, 2, AHEAD + 24)])
PLAN_LAST = plan([spread(LATE, range(0, AHEAD))], [(0, 3, AHEAD)])
PLAN_BEFORE = [units_of(0, 0) + [(0, FOLD, 0)] + units_of(0, 1)[:8] + [(0, TURN, 0), (0, SPLIT, 0)] + units_of(0, 1)[8:]]
PLAN_FIRST = plan([spread(units_of(0, 2), range(0, 9)), spread(units_of(0, 3), range(9, 21)),
                   spread(units_of(1, 0, 1, 2), range(21, NR - 2)), spread(EARLY[OF_CHUNK[3][0]:], range(NR - 2, NR))],
                  [(0, 1, 0), (0, 2, 9), (0, 3, 21), (1, 0, 24), (1, 1, 30), (1, 2, NR - 2)])


def max_banks(this, before, ahead):
    mine = [e for events in this for e in events if e[1] in (UNIT, TURN)]
    theirs = [e for events in before for e in events if e[1] in (UNIT, TURN)]
    out = {}
    for k, e in enumerate(mine):
        bank = (len(mine) - 1 - k) % M_BANKS
        last = None
        if k >= M_BANKS:
            last = mine[k - M_BANKS]
        elif theirs:
            dg, kind, n = theirs[len(theirs) - 1 - bank]
            last = (dg - ahead, kind, n)
        out[e] = bank, last
    return out


BANKS_BEFORE = max_banks(PLAN_BEFORE, [], 0)
BANKS_FIRST = max_banks(PLAN_FIRST, PLAN_BEFORE, 0)
BANKS_MID = max_banks(PLAN_MID, PLAN_MID, 1)
BANKS_LAST = max_banks(PLAN_LAST, PLAN_MID, 1)


def plan_of(g, last):
    if last:
        return PLAN_LAST, BANKS_LAST
    if isinstance(g, int) and g == 0:
        return PLAN_FIRST, BANKS_FIRST
    return PLAN_MID, BANKS_MID


LEAVE_AT = {(LAST_ROUND[c] + 1) % NR: ((LAST_ROUND[c] + 1) // NR, c) for c in range(QC)}
QUARTERS = 4
INVERT_AT = {(LAST_ROUND[c] + 2 + k) % NR: ((LAST_ROUND[c] + 2 + k) // NR, c, k)
             for c in range(QC) for k in range(QUARTERS)}
Y_BEFORE_PAIR = {min([p for p in range(NPAIR) if PAIR_LAST[p] > (LAST_ROUND[c] + 2 + QUARTERS) % NR] or [NPAIR]):
                 ((LAST_ROUND[c] + 2 + QUARTERS) // NR, c) for c in range(QC)}


class Memory:
    pass


def wait_past(eng, sem, count):
    if not isinstance(count, int) or count > 0:
        eng.wait_ge(sem, count)


def earlier_user(u, ring, per_group):
    if u >= ring:
        return 0, u - ring
    return 1, max(v for v in range(per_group) if v % ring == u % ring)


def prenorm_alibi_attention_plus_top1_experts(nc, x, w_qkv, w_o, w_g, w_e, b_e, out):
    m = Memory()
    m.x, m.out = x.rearrange("b s d -> (b s) d"), out.rearrange("b s d -> (b s) d")
    m.w_qkv, m.w_o, m.w_g, m.w_e, m.b_e = w_qkv, w_o, w_g, w_e, b_e

    m.q_hi_d = nc.dram_tensor("q_hi_d", [G, P, S], F32).ap()
    m.q_lo_d = nc.dram_tensor("q_lo_d", [G, P, S], F32).ap()
    m.k_hi_d = nc.dram_tensor("k_hi_d", [G, P, S], F32).ap()
    m.k_lo_d = nc.dram_tensor("k_lo_d", [G, P, S], F32).ap()
    m.v_d = nc.dram_tensor("v_d", [N, D], F32).ap()
    m.xn_d = nc.dram_tensor("xn_d", [N, D], F32).ap()
    m.y_d = nc.dram_tensor("y_d", [G, P, S], F32).ap()
    m.slot_x_d = nc.dram_tensor("slot_x_d", [SLOTS, D], F32).ap()
    m.slot_y_d = nc.dram_tensor("slot_y_d", [SLOT_TILES * P, D], F32).ap()
    m.k_rows_d = nc.dram_tensor("k_rows_d", [4, H, S], F32).ap()
    m.q_rows_d = nc.dram_tensor("q_rows_d", [6, HG, S], F32).ap()

    with ExitStack() as held:
        def sb(name, shape, dt):
            return held.enter_context(nc.sbuf_tensor(name, shape, dt))

        m.ident = sb("ident", [P, P], F32)
        m.ident_bf = sb("ident_bf", [P, P], BF16)
        m.mask_qk = sb("mask_qk", [P, P], BF16)
        m.mask_kq = sb("mask_kq", [P, P], BF16)
        m.ones = sb("ones", [P, DH], F32)
        m.slot = sb("slot", [P, NT], I32)
        m.gate = sb("gate", [P, NT], F32)
        m.tile_expert = sb("tile_expert", [1, SLOT_TILES + 1], I32)
        m.alibi_bias = sb("alibi_bias", [P, H * QT], F32)
        m.max_shift = sb("max_shift", [P, H * QT], F32)
        project_and_route(nc, m)
        with ExitStack() as c:
            with nc.sbuf_tensor("w_nat", [P, 2, E, KC, D], F32) as m.w_nat:
                pass
            m.q_aug = c.enter_context(nc.sbuf_tensor("q_aug", [P, 2, HG, S], F32R))
            m.k_aug = c.enter_context(nc.sbuf_tensor("k_aug", [P, 2, HG, S], F32R))
            attend(nc, m)
            right = lambda n, s, d: held.enter_context(nc.sbuf_tensor(n, s, d, side="right"))
            m.wo_hi = right("wo_hi", [P, KC, D], F32R)
            m.wo_lo = right("wo_lo", [P, KC, D], F32R)
            m.yT = right("yT", [P, Y_BUFS, KC, CH], F32)
            run_experts(nc, m)
        combine(nc, m)


def project_and_route(nc, m):
    NQK = 2 * D // P
    NG = NQK + TPC
    BANKS = 4
    AHEAD = 6
    NV = 12
    EIGHTS = P // H
    KEYS = S // EIGHTS
    ZEROED = 2
    with ExitStack() as c:
        sb = lambda n, s, d: c.enter_context(nc.sbuf_tensor(n, s, d))
        pb = lambda n, s, d: c.enter_context(nc.psum_tensor(n, s, d))
        sem = lambda n: c.enter_context(nc.semaphore(n))
        w_f = sb("w_f", [P, KC, 3 * D], F32)
        w_hi = sb("w_hi", [P, KC, 3 * D], F32R)
        w_lo = sb("w_lo", [P, KC, 3 * D], F32R)
        wg_f = sb("wg_f", [P, KC, E], F32)
        wg_parts = sb("wg_parts", [P, KC, P], F32R)
        logT = sb("logT", [2 * E, N], F32)
        xt = sb("xt", [P, 2, TPC, D], F32)
        xn = sb("xn", [P, 2, TPC, D], F32)
        xT_hi = sb("xT_hi", [P, 2, KC, CH], F32R)
        xT_lo = sb("xT_lo", [P, 2, KC, CH], F32R)
        st_hi = sb("st_hi", [P, BANKS, CH], F32R)
        st_lo = sb("st_lo", [P, BANKS, CH], F32R)
        st_v = sb("st_v", [P, 2, D], F32)
        stats = sb("stats", [P, TPC, 6], F32)
        mean2 = sb("mean2", [P, TPC], F32)
        diff = sb("diff", [P, TPC], F32)
        spread = sb("spread", [P, TPC], F32)
        mean = sb("mean", [P, TPC], F32)
        diff_sq = sb("diff_sq", [P, TPC], F32)
        between = sb("between", [P, TPC], F32)
        var_eps = sb("var_eps", [P, TPC], F32)
        root = sb("root", [P, TPC], F32)
        inv = sb("inv", [P, TPC], F32)
        inv_sq = sb("inv_sq", [P, TPC], F32)
        near_one = sb("near_one", [P, TPC], F32)
        factor = sb("factor", [P, TPC], F32)
        rstd = sb("rstd", [P, TPC], F32)
        cols_row = sb("cols_row", [1, 2, P], F32)
        slope_col = sb("slope_col", [P, 1], F32)
        passed_col = sb("passed_col", [P, 1], F32)
        key_i = sb("key_i", [P, KEYS], I32)
        key_all = sb("key_all", [P, KEYS], F32)
        key_f = sb("key_f", [P, KEYS], F32)
        sk = sb("sk", [P, KEYS], F32)
        sk_hi = sb("sk_hi", [P, KEYS], F32R)
        sk_lo = sb("sk_lo", [P, KEYS], F32R)
        one_f = sb("one_f", [P, KEYS], F32)
        zero_f = sb("zero_f", [P, ZEROED * D], F32)
        rel_i = sb("rel_i", [P, QT], I32)
        rel_f = sb("rel_f", [P, QT], F32)
        first_i = sb("first_i", [P, QT], I32)
        first_f = sb("first_f", [P, QT], F32)
        lg = sb("lg", [P, NT, E], F32)
        lg2 = sb("lg2", [P, NT, E], F32)
        ex = sb("ex", [P, NT, E], F32)
        probs = sb("probs", [P, NT, E], F32)
        cand = sb("cand", [P, NT, E], F32)
        hot = sb("hot", [P, NT, E], F32)
        hot_bf = sb("hot_bf", [P, NT, E], BF16)
        totals = sb("totals", [P, NT, E], F32)
        run = [sb("run0", [P, NT, E], F32), sb("run1", [P, NT, E], F32)]
        place = sb("place", [P, NT, E], F32)
        col = sb("col", [P, NT], F32)
        rcp = sb("rcp", [P, NT], F32)
        rank_i = sb("rank_i", [P, E], I32)
        rank_f = sb("rank_f", [P, E], F32)
        full_i = sb("full_i", [P, NT], I32)
        full_f = sb("full_f", [P, NT], F32)
        tile_i = sb("tile_i", [P, SLOT_TILES], I32)
        tile_f = sb("tile_f", [P, SLOT_TILES], F32)
        more_than = sb("more_than", [P, E, NT], F32)
        tiles = [sb("tiles0", [P, E], F32), sb("tiles1", [P, E], F32)]
        start = sb("start", [P, E], F32)
        start_row = sb("start_row", [P, E], F32)
        below = sb("below", [P, SLOT_TILES, E], F32)
        expert = sb("expert", [P, SLOT_TILES], F32)
        tri = sb("tri", [P, P], BF16)
        ones_bf = sb("ones_bf", [P, P], BF16)
        group_ps = pb("group_ps", [P, BANKS, CH], F32)
        trans_ps = pb("trans_ps", [P, 2, CH], F32)
        router_ps = pb("router_ps", [P, CH], F32)
        log_ps = pb("log_ps", [P, NT, 2 * E], F32)
        rank_ps, total_ps = (trans_ps[:, b, 0:NT * E].rearrange("p (n e) -> p n e", e=E) for b in (0, 1))

        x_loaded = [sem("x_loaded0"), sem("x_loaded1")]
        x_first = [sem(f"x_first{a}") for a in range(TPC - 1)]
        stats_done, var_done, root_done, xn_done = sem("stats_done"), sem("var_done"), sem("root_done"), sem("xn_done")
        xn_stored = [sem("xn_stored0"), sem("xn_stored1")]
        transposed, tr_hi_done, tr_lo_done = sem("transposed"), sem("tr_hi_done"), sem("tr_lo_done")
        router_done, router_copied = sem("router_done"), sem("router_copied")
        group_done, copied, lo_done = sem("group_done"), sem("copied"), sem("lo_done")
        hi_stored = [sem(f"hi_stored{i}") for i in range(BANKS)]
        lo_stored = [sem(f"lo_stored{i}") for i in range(BANKS)]
        v_stored = [sem("v_stored0"), sem("v_stored1")]
        w_loaded, wg_loaded = [sem(f"w_loaded{k}") for k in range(KC)], sem("wg_loaded")
        w_hi_done, w_lo_done, wg_done = sem("w_hi_done"), sem("w_lo_done"), sem("wg_done")
        blank, ident_done, cols_set, cols_loaded, filled, tables = (
            sem("blank"), sem("ident_done"), sem("cols_set"), sem("cols_loaded"), sem("filled"), sem("tables"))
        rows_stored, zeros_stored = sem("rows_stored"), sem("zeros_stored")
        made, logits_ready, shifted, exp_done, step_done, hot_ready, counted = (
            sem("made"), sem("logits_ready"), sem("shifted"), sem("exp_done"), sem("step_done"), sem("hot_ready"),
            sem("counted"))

        def chunk_pairs(eng, body):
            body(0, 0, True)
            body(0, 1, True)
            with eng.Fori(1, NCH // 2 - 1) as i:
                body(i, 0, True)
                body(i, 1, True)
            body(NCH // 2 - 1, 0, True)
            body(NCH // 2 - 1, 1, False)

        with nc.Block() as block:
            @block.sync
            def _(sp):
                x_c = m.x.rearrange("(c a p) d -> c p a d", a=TPC, p=P)
                xn_c = m.xn_d.rearrange("(c a p) d -> c p a d", a=TPC, p=P)
                v_c = m.v_d.rearrange("(n p) d -> n p d", p=P)
                for a in range(TPC):
                    sp.dma_start(xt[:, 0, a], x_c[0][:, a]).then_inc(x_loaded[0] if a == TPC - 1 else x_first[a], 16)
                for k in range(KC):
                    sp.dma_start(w_f[:, k], m.w_qkv[k * P:(k + 1) * P, :]).then_inc(w_loaded[k], 16)
                    if k == 0:
                        sp.dma_start(wg_f[:], m.w_g.rearrange("(k p) n -> p k n", p=P)).then_inc(wg_loaded, 16)
                sp.dma_start(xt[:, 1], x_c[1]).then_inc(x_loaded[1], 16)

                def body(i, half, more):
                    ch = 2 * i + half
                    batch, cc = i // (QC // 2), (i % (QC // 2)) * 2 + half
                    sp.wait_ge(xn_done, (ch + 1) * TPC)
                    sp.dma_start(xn_c[ch], xn[:, half]).then_inc(xn_stored[half], 16)
                    if not isinstance(i, int) or i < NCH // 2 - 1:
                        sp.dma_start(xt[:, half], x_c[ch + 2]).then_inc(x_loaded[half], 16)
                    for e in range(NQK):
                        hi_d, lo_d = (m.q_hi_d, m.q_lo_d) if e < NQK // 2 else (m.k_hi_d, m.k_lo_d)
                        g = batch * GB + e % GB
                        sp.wait_ge(copied, ch * NG + e + 1)
                        sp.dma_start(hi_d[g, :, bass.ts(cc, CH)], st_hi[:, e % BANKS].bitcast(F32)).then_inc(hi_stored[e % BANKS], 16)
                        sp.wait_ge(lo_done, ch * NQK + e + 1)
                        sp.dma_start(lo_d[g, :, bass.ts(cc, CH)], st_lo[:, e % BANKS].bitcast(F32)).then_inc(lo_stored[e % BANKS], 16)
                    for a in range(TPC):
                        sp.wait_ge(copied, ch * NG + NQK + a + 1)
                        sp.dma_start(v_c[ch * TPC + a], st_v[:, a % 2]).then_inc(v_stored[a % 2], 16)

                chunk_pairs(sp, body)
                for s in (*hi_stored, *lo_stored):
                    sp.wait_ge(s, 16 * NCH * NQK // BANKS)
                for s in v_stored:
                    sp.wait_ge(s, 16 * NCH * TPC // 2)
                for s in xn_stored:
                    sp.wait_ge(s, 16 * NCH // 2)

            @block.gpsimd
            def _(pool):
                for t in (m.ident, m.ident_bf, m.mask_qk, m.mask_kq):
                    nc.gpsimd.memset(t[:], 0.0).then_inc(blank, 1)
                pool.wait_ge(blank, 4)
                for t in (m.ident, m.ident_bf):
                    nc.gpsimd.affine_select(out=t[:], in_=t[:], compare_op=ALU.not_equal, fill=1.0, base=0,
                                            pattern=[[-1, P]], channel_multiplier=1).then_inc(ident_done, 1)
                nc.gpsimd.affine_select(out=m.mask_qk[:], in_=m.mask_qk[:], compare_op=ALU.is_ge, fill=NEG, base=0,
                                        pattern=[[-1, P]], channel_multiplier=1)
                nc.gpsimd.affine_select(out=m.mask_kq[:], in_=m.mask_kq[:], compare_op=ALU.is_ge, fill=NEG, base=0,
                                        pattern=[[1, P]], channel_multiplier=-1)
                nc.gpsimd.memset(m.ones[:], 1.0)
                for h in range(H):
                    here = slice(h * EIGHTS, (h + 1) * EIGHTS)
                    nc.gpsimd.memset(cols_row[0:1, 0, here], SLOPES[h]).then_inc(cols_set, 1)
                    nc.gpsimd.memset(cols_row[0:1, 1, here], float(h * S)).then_inc(cols_set, 1)
                pool.wait_ge(cols_set, 2 * H)
                pool.dma_start(slope_col[:, 0:1], cols_row[0:1, 0, :]).then_inc(cols_loaded, 16)
                pool.dma_start(passed_col[:, 0:1], cols_row[0:1, 1, :]).then_inc(cols_loaded, 16)
                nc.gpsimd.memset(one_f[:], 1.0).then_inc(filled, 1)
                nc.gpsimd.memset(zero_f[:], 0.0).then_inc(filled, 1)
                nc.gpsimd.memset(tri[:], 1.0).then_inc(made, 1)
                nc.gpsimd.memset(ones_bf[:], 1.0).then_inc(made, 1)
                nc.gpsimd.iota(rank_i[:], [[-1, E]], base=E, channel_multiplier=0).then_inc(made, 1)
                nc.gpsimd.iota(full_i[:], [[P, NT]], base=0, channel_multiplier=0).then_inc(made, 1)
                nc.gpsimd.iota(tile_i[:], [[1, SLOT_TILES]], base=0, channel_multiplier=0).then_inc(made, 1)
                pool.wait_ge(made, 5)
                nc.gpsimd.affine_select(out=tri[:], in_=tri[:], compare_op=ALU.is_gt, fill=0.0, base=0,
                                        pattern=[[1, P]], channel_multiplier=-1).then_inc(made, 1)
                nc.gpsimd.iota(key_i[:], [[1, KEYS]], base=0, channel_multiplier=KEYS).then_inc(tables, 1)
                nc.gpsimd.iota(rel_i[:], [[P, QT]], base=-P * (QT - TPC), channel_multiplier=1).then_inc(tables, 1)
                nc.gpsimd.iota(first_i[:], [[CH, QC], [0, TPC]], base=0, channel_multiplier=0).then_inc(tables, 1)
                pool.wait_ge(tables, 3)
                nc.gpsimd.tensor_copy(key_all[:], key_i[:]).then_inc(tables, 1)
                nc.gpsimd.tensor_copy(rel_f[:], rel_i[:]).then_inc(tables, 1)
                nc.gpsimd.tensor_copy(first_f[:], first_i[:]).then_inc(tables, 1)
                pool.wait_ge(tables, 6)
                pool.wait_ge(cols_loaded, 32)
                nc.gpsimd.tensor_scalar(key_f[:], key_all[:], passed_col[:, 0:1], None, ALU.subtract).then_inc(tables, 1)
                pool.wait_ge(tables, 7)
                nc.gpsimd.tensor_scalar(sk[:], key_f[:], slope_col[:, 0:1], None, ALU.mult).then_inc(tables, 1)
                pool.wait_ge(tables, 8)
                nc.gpsimd.tensor_copy(sk_hi[:], sk[:]).then_inc(tables, 1)
                pool.wait_ge(tables, 9)
                nc.gpsimd.tensor_tensor(sk_lo[:], sk[:], sk_hi[:].bitcast(F32), ALU.subtract).then_inc(tables, 1)
                pool.wait_ge(tables, 10)
                shift = m.max_shift[:].rearrange("p (g c h i) -> p g h c i", g=GB, c=QC, h=HG)
                for h in range(H):
                    nc.gpsimd.tensor_scalar(m.alibi_bias[:, bass.ts(h, QT)], rel_f[:], SLOPES[h], None, ALU.mult)
                    nc.gpsimd.tensor_scalar(shift[:, h // HG, h % HG], first_f[:].rearrange("p (c i) -> p c i", c=QC),
                                            SLOPES[h], None, ALU.mult)
                pool.wait_ge(group_done, 1)
                pool.wait_ge(filled, 2)
                q_row, k_row = (t.rearrange("r h (s n) -> r (h s) n", n=KEYS) for t in (m.q_rows_d, m.k_rows_d))
                for r in (2, 3):
                    pool.dma_start(k_row[r], one_f[:]).then_inc(rows_stored, 16)
                for r in (0, 1):
                    pool.dma_start(q_row[r], one_f[0:HG * EIGHTS]).then_inc(rows_stored, 16)
                for r in (2, 3, 4, 5):
                    pool.dma_start(q_row[r], zero_f[0:HG * EIGHTS, 0:KEYS]).then_inc(rows_stored, 16)
                pool.dma_start(k_row[0], sk_hi[:].bitcast(F32)).then_inc(rows_stored, 16)
                pool.dma_start(k_row[1], sk_lo[:].bitcast(F32)).then_inc(rows_stored, 16)
                slots = m.slot_x_d.rearrange("(n p) d -> p n d", p=P)
                for n in range(0, SLOTS // P, ZEROED):
                    if n // ZEROED % 4 == 0:
                        pool.wait_ge(group_done, NG * (1 + n // (4 * ZEROED)))
                    k = min(ZEROED, SLOTS // P - n)
                    pool.dma_start(slots[:, n:n + k, :], zero_f[:, 0:k * D].rearrange("p (n d) -> p n d", d=D)).then_inc(
                        zeros_stored, 16)
                pool.wait_ge(zeros_stored, 16 * len(range(0, SLOTS // P, ZEROED)))
                pool.wait_ge(rows_stored, 16 * 10)

            @block.vector
            def _(dve):
                def norm(ch, i, half):
                    for a in range(TPC):
                        if isinstance(ch, int) and ch == 0 and a < TPC - 1:
                            dve.wait_ge(x_first[a], 16)
                        elif a == TPC - 1 or not (isinstance(ch, int) and ch == 0):
                            dve.wait_ge(x_loaded[half], 16 * (i + 1))
                        nc.vector.bn_stats(stats[:, a], xt[:, half, a]).then_inc(stats_done, 1)
                    v = ch * NV
                    dve.wait_ge(stats_done, (ch + 1) * TPC)
                    nc.vector.tensor_tensor(mean2[:], stats[:, :, 1], stats[:, :, 4], ALU.add).then_inc(var_done, 1)
                    nc.vector.tensor_tensor(diff[:], stats[:, :, 1], stats[:, :, 4], ALU.subtract).then_inc(var_done, 1)
                    nc.vector.tensor_tensor(spread[:], stats[:, :, 2], stats[:, :, 5], ALU.add).then_inc(var_done, 1)
                    dve.wait_ge(var_done, v + 3)
                    nc.vector.tensor_scalar(mean[:], mean2[:], 0.5, None, ALU.mult).then_inc(var_done, 1)
                    nc.vector.tensor_tensor(diff_sq[:], diff[:], diff[:], ALU.mult).then_inc(var_done, 1)
                    dve.wait_ge(var_done, v + 5)
                    nc.vector.tensor_scalar(between[:], diff_sq[:], 0.25, EPS, ALU.mult, ALU.add).then_inc(var_done, 1)
                    dve.wait_ge(var_done, v + 6)
                    nc.vector.scalar_tensor_tensor(var_eps[:], spread[:], 1.0 / D, between[:], ALU.mult,
                                                   ALU.add).then_inc(var_done, 1)
                    dve.wait_ge(root_done, ch + 1)
                    nc.vector.reciprocal(inv[:], root[:]).then_inc(var_done, 1)
                    dve.wait_ge(var_done, v + 8)
                    nc.vector.tensor_tensor(inv_sq[:], inv[:], inv[:], ALU.mult).then_inc(var_done, 1)
                    dve.wait_ge(var_done, v + 9)
                    nc.vector.tensor_tensor(near_one[:], inv_sq[:], var_eps[:], ALU.mult).then_inc(var_done, 1)
                    dve.wait_ge(var_done, v + 10)
                    nc.vector.tensor_scalar(factor[:], near_one[:], -0.5, 1.5, ALU.mult, ALU.add).then_inc(var_done, 1)
                    dve.wait_ge(var_done, v + 11)
                    nc.vector.tensor_tensor(rstd[:], inv[:], factor[:], ALU.mult).then_inc(var_done, 1)
                    dve.wait_ge(var_done, v + 12)
                    wait_past(dve, xn_stored[half], 16 * i)
                    wait_past(dve, transposed, (ch - 1) * KC)
                    for a in range(TPC):
                        nc.vector.tensor_scalar(xn[:, half, a], xt[:, half, a], mean[:, a:a + 1], rstd[:, a:a + 1],
                                                ALU.subtract, ALU.mult).then_inc(xn_done, 1)

                def low_parts(ch, half):
                    for k in range(KC):
                        dve.wait_ge(tr_hi_done, ch * KC + k + 1)
                        nc.vector.tensor_tensor(xT_lo[:, half, k], trans_ps[:, k % 2], xT_hi[:, half, k].bitcast(F32),
                                                ALU.subtract).then_inc(tr_lo_done, 1)

                steps = [0]

                def step(ins):
                    steps[0] += 1
                    ins.then_inc(step_done, 1)
                    dve.wait_ge(step_done, steps[0])

                def by_tile(a):
                    return a.unsqueeze(2).to_broadcast([P, NT, E])

                v = nc.vector

                def shift_logits():
                    dve.wait_ge(made, 6)
                    step(v.tensor_copy(rank_f[:], rank_i[:]))
                    step(v.tensor_copy(full_f[:], full_i[:]))
                    dve.wait_ge(logits_ready, 1)
                    step(v.tensor_copy(lg2[:], log_ps[:, :, E:2 * E]))
                    step(v.tensor_tensor(lg[:], log_ps[:, :, 0:E], lg2[:], ALU.add))
                    step(v.tensor_reduce(col[:], lg[:], AX.X, ALU.max))
                    v.tensor_tensor(lg[:], lg[:], by_tile(col[:]), ALU.subtract).then_inc(shifted, 1)

                def gates():
                    dve.wait_ge(exp_done, 1)
                    step(v.tensor_reduce(col[:], ex[:], AX.X, ALU.add))
                    step(v.reciprocal(rcp[:], col[:]))
                    step(v.tensor_tensor(probs[:], ex[:], by_tile(rcp[:]), ALU.mult))
                    step(v.tensor_reduce(m.gate[:], probs[:], AX.X, ALU.max))

                def first_of_largest():
                    step(v.tensor_tensor(cand[:], probs[:], by_tile(m.gate[:]), ALU.is_equal))
                    step(v.tensor_tensor(cand[:], cand[:], rank_f[:].unsqueeze(1).to_broadcast([P, NT, E]), ALU.mult))
                    step(v.tensor_reduce(col[:], cand[:], AX.X, ALU.max))
                    step(v.tensor_tensor(hot[:], cand[:], by_tile(col[:]), ALU.is_equal))
                    v.tensor_copy(hot_bf[:], hot[:]).then_inc(hot_ready, 1)

                def slots():
                    dve.wait_ge(counted, 1)
                    step(v.tensor_copy(totals[:], total_ps))
                    step(v.tensor_copy(run[0][:], totals[:]))
                    a, b, d = 0, 1, 1
                    while d < NT:
                        step(v.tensor_copy(run[b][:, 0:d], run[a][:, 0:d]))
                        step(v.tensor_tensor(run[b][:, d:NT], run[a][:, d:NT], run[a][:, 0:NT - d], ALU.add))
                        a, b, d = b, a, 2 * d
                    counts = run[a][:, NT - 1]
                    step(v.tensor_tensor(more_than[:], counts.unsqueeze(2).to_broadcast([P, E, NT]),
                                         full_f[:].unsqueeze(1).to_broadcast([P, E, NT]), ALU.is_gt))
                    step(v.tensor_reduce(tiles[0][:], more_than[:], AX.X, ALU.add))
                    step(v.tensor_copy(start[:], tiles[0][:]))
                    ta, tb, d = 0, 1, 1
                    while d < E:
                        step(v.tensor_copy(tiles[tb][:, 0:d], tiles[ta][:, 0:d]))
                        step(v.tensor_tensor(tiles[tb][:, d:E], tiles[ta][:, d:E], tiles[ta][:, 0:E - d], ALU.add))
                        ta, tb, d = tb, ta, 2 * d
                    step(v.tensor_tensor(start[:], tiles[ta][:], start[:], ALU.subtract))
                    step(v.tensor_scalar(start_row[:], start[:], float(P), None, ALU.mult))
                    step(v.tensor_tensor(place[:], run[a][:], totals[:], ALU.subtract))
                    step(v.tensor_tensor(place[:], rank_ps, place[:], ALU.add))
                    step(v.tensor_tensor(place[:], place[:], start_row[:].unsqueeze(1).to_broadcast([P, NT, E]), ALU.add))
                    step(v.tensor_tensor(place[:], place[:], hot[:], ALU.mult))
                    step(v.tensor_reduce(col[:], place[:], AX.X, ALU.add))
                    step(v.tensor_copy(m.slot[:], col[:]))
                    step(v.tensor_copy(tile_f[:], tile_i[:]))
                    step(v.tensor_tensor(below[:], start[:].unsqueeze(1).to_broadcast([P, SLOT_TILES, E]),
                                         tile_f[:].unsqueeze(2).to_broadcast([P, SLOT_TILES, E]), ALU.is_le))
                    step(v.tensor_reduce(expert[:], below[:], AX.X, ALU.add))
                    step(v.tensor_scalar(expert[:], expert[:], -1.0, None, ALU.add))
                    step(v.tensor_copy(m.tile_expert[0:1, 0:SLOT_TILES], expert[0:1, :]))

                def route_before(e):
                    if e == 2:
                        shift_logits()
                    elif e == 4:
                        gates()
                    elif e == 5:
                        first_of_largest()

                def body(i, half, more):
                    ch = 2 * i + half
                    if more:
                        norm(ch + 1, i + half, 1 - half)
                    for e in range(NQK):
                        if e == AHEAD and more:
                            low_parts(ch + 1, 1 - half)
                        if not more:
                            route_before(e)
                        dve.wait_ge(copied, ch * NG + e + 1)
                        wait_past(dve, lo_stored[e % BANKS], 16 * (ch * (NQK // BANKS) + e // BANKS))
                        nc.vector.scalar_tensor_tensor(st_lo[:, e % BANKS], group_ps[:, e % BANKS],
                                                       SCALE if e < NQK // 2 else 1.0, st_hi[:, e % BANKS].bitcast(F32),
                                                       ALU.mult, ALU.subtract).then_inc(lo_done, 1)

                nc.vector.memset(wg_parts[:].bitcast(F32), 0.0).then_inc(wg_done, 1)
                norm(0, 0, 0)
                low_parts(0, 0)
                dve.wait_ge(wg_loaded, 16)
                dve.wait_ge(wg_done, 1)
                nc.vector.tensor_copy(wg_parts[:, :, 0:E], wg_f[:]).then_inc(wg_done, 1)
                dve.wait_ge(wg_done, 2)
                nc.vector.tensor_tensor(wg_parts[:, :, E:2 * E], wg_f[:], wg_parts[:, :, 0:E].bitcast(F32),
                                        ALU.subtract).then_inc(wg_done, 1)
                for k in range(KC):
                    dve.wait_ge(w_hi_done, k + 1)
                    nc.vector.tensor_tensor(w_lo[:, k], w_f[:, k], w_hi[:, k].bitcast(F32), ALU.subtract).then_inc(w_lo_done, 1)
                chunk_pairs(dve, body)
                slots()

            @block.scalar
            def _(act):
                def root_of(ch):
                    act.wait_ge(var_done, ch * NV + 7)
                    nc.scalar.activation(root[:], var_eps[:], ACT.Sqrt).then_inc(root_done, 1)

                def high_parts(ch, half):
                    for k in range(KC):
                        act.wait_ge(transposed, ch * KC + k + 1)
                        nc.scalar.activation(xT_hi[:, half, k], trans_ps[:, k % 2], ACT.Copy).then_inc(tr_hi_done, 1)

                def body(i, half, more):
                    ch = 2 * i + half
                    if more:
                        root_of(ch + 1)
                    act.wait_ge(router_done, ch + 1)
                    nc.scalar.activation(logT[:, bass.ts(ch, CH)], router_ps[0:2 * E, :], ACT.Copy).then_inc(
                        router_copied, 1)
                    for e in range(NQK):
                        if e == AHEAD and more:
                            high_parts(ch + 1, 1 - half)
                        if not more and e == 3:
                            act.wait_ge(shifted, 1)
                            nc.scalar.activation(ex[:], lg[:], ACT.Exp).then_inc(exp_done, 1)
                        act.wait_ge(group_done, ch * NG + e + 1)
                        wait_past(act, hi_stored[e % BANKS], 16 * (ch * (NQK // BANKS) + e // BANKS))
                        nc.scalar.activation(st_hi[:, e % BANKS], group_ps[:, e % BANKS], ACT.Copy,
                                             scale=SCALE if e < NQK // 2 else 1.0).then_inc(copied, 1)
                    for a in range(TPC):
                        act.wait_ge(group_done, ch * NG + NQK + a + 1)
                        wait_past(act, v_stored[a % 2], 16 * (ch * (TPC // 2) + a // 2))
                        nc.scalar.activation(st_v[:, a % 2], group_ps[:, (NQK + a) % BANKS], ACT.Copy).then_inc(copied, 1)

                root_of(0)
                high_parts(0, 0)
                for k in range(KC):
                    act.wait_ge(w_loaded[k], 16)
                    nc.scalar.activation(w_hi[:, k], w_f[:, k], ACT.Copy).then_inc(w_hi_done, 1)
                chunk_pairs(act, body)

            @block.tensor
            def _(pe):
                def transposes(ch, half):
                    pe.wait_ge(xn_done, (ch + 1) * TPC)
                    for k in range(KC):
                        wait_past(pe, tr_lo_done, ch * KC + k - 1)
                        for a in range(TPC):
                            last = nc.tensor.transpose(trans_ps[:, k % 2, a * P:(a + 1) * P],
                                                       xn[:, half, a, k * P:(k + 1) * P], m.ident[:])
                        last.then_inc(transposed, 1)

                def body(i, half, more):
                    ch = 2 * i + half
                    pe.wait_ge(tr_lo_done, (ch + 1) * KC)
                    wait_past(pe, router_copied, ch)
                    for k in range(KC):
                        for part in (xT_hi, xT_lo):
                            last = nc.tensor.matmul(router_ps[:], wg_parts[:, k], part[:, half, k],
                                                    start=(k == 0 and part is xT_hi), stop=(k == KC - 1 and part is xT_lo))
                    last.then_inc(router_done, 1)
                    for n in range(NG):
                        if n == AHEAD and more:
                            transposes(ch + 1, 1 - half)
                        if n == 1 and not more:
                            pe.wait_ge(router_copied, NCH)
                            for t in range(NT):
                                turned = nc.tensor.transpose(log_ps[:, t], logT[:, t * P:(t + 1) * P], m.ident[0:2 * E, 0:2 * E])
                            turned.then_inc(logits_ready, 1)
                        if n == NQK and not more:
                            pe.wait_ge(hot_ready, 1)
                            nc.tensor.matmul(rank_ps, tri[:], hot_bf[:], start=True, stop=True)
                            nc.tensor.matmul(total_ps, ones_bf[:], hot_bf[:], start=True, stop=True).then_inc(counted, 1)
                        if n == 0:
                            wait_past(pe, copied, ch * NG)
                        elif n >= BANKS:
                            pe.wait_ge(lo_done, ch * NQK + n - BANKS + 1)
                        for k in range(KC):
                            for p, (x_part, w_part) in enumerate(((xT_hi, w_hi), (xT_lo, w_hi), (xT_hi, w_lo))):
                                if n < NQK:
                                    lhs, rhs = w_part[:, k, n * P:(n + 1) * P], x_part[:, half, k]
                                else:
                                    a = n - NQK
                                    lhs, rhs = x_part[:, half, k, a * P:(a + 1) * P], w_part[:, k, 2 * D:3 * D]
                                last = nc.tensor.matmul(group_ps[:, n % BANKS], lhs, rhs,
                                                        start=(k == 0 and p == 0), stop=(k == KC - 1 and p == 2))
                        last.then_inc(group_done, 1)

                pe.wait_ge(ident_done, 1)
                transposes(0, 0)
                pe.wait_ge(wg_done, 3)
                pe.wait_ge(w_lo_done, KC)
                chunk_pairs(pe, body)




def attend(nc, m):
    with ExitStack() as c:
        sb = lambda n, s, d: c.enter_context(nc.sbuf_tensor(n, s, d))
        pb = lambda n, s, d: c.enter_context(nc.psum_tensor(n, s, d))
        sem = lambda n: c.enter_context(nc.semaphore(n))
        q_aug, k_aug = m.q_aug, m.k_aug
        v_sb = sb("v_sb", [P, 2, QT, P], F32)
        probs = sb("probs_sb", [P, P_SLOTS, HG, CH], F32)
        pair_sum = sb("pair_sum", [P, 2, HG, CH], F32)
        bias = sb("bias", [P, 2, HG * QT], F32)
        part_max = sb("part_max", [P, QT * HG, QC], F32)
        row_max = sb("row_max", [P, HG * TPC], F32)
        neg_max = sb("neg_max", [P, P], F32)
        max_hi = sb("max_hi", [HG * TPC, 2, P], F32R)
        max_lo = sb("max_lo", [HG * TPC, 2, P], F32R)
        acc_sb = sb("acc_sb", [P, 2, 2, CH], F32)
        y_sb, den_sb = acc_sb[:, :, 0], acc_sb[:, :, 1]
        score_ps = pb("score_ps", [P, S_BANKS, CH], F32)
        max_ps = pb("max_ps", [P, M_BANKS, CH], F32)
        acc_ps = pb("acc_ps", [P, 2, CH], F32)
        y_ps, den_ps = acc_ps[:, 0], acc_ps[:, 1]

        aug_loaded = [sem("aug_loaded0"), sem("aug_loaded1")]
        first_loaded = [sem(f"first_loaded{cc}") for cc in range(QC - 1)]
        v_loaded = [sem("v_loaded0"), sem("v_loaded1")]
        max_rows_loaded = [sem("max_rows_loaded0"), sem("max_rows_loaded1")]
        y_stored = [sem("y_stored0"), sem("y_stored1")]
        max_scored, max_taken = sem("max_scored"), sem("max_taken")
        max_blank, folded, neg_done, max_turned, max_hi_done, max_lo_done = (
            sem("max_blank"), sem("folded"), sem("neg_done"), sem("max_turned"), sem("max_hi_done"), sem("max_lo_done"))
        bias_ready, scored, exp_done, pv_done, pair_added, pair_used = (
            sem("bias_ready"), sem("scored"), sem("probs_ready"), sem("pv_done"), sem("pair_added"), sem("pair_used"))
        experts_loaded = sem("experts_loaded")
        accs_left, inverted, y_done = sem("accs_left"), sem("inverted"), sem("y_done")
        xn_loaded, slots_stored = [sem("xn_loaded0"), sem("xn_loaded1")], sem("slots_stored")
        XN_TILES = 4
        AUG = 16 * 8
        MAX_ROWS = 16 * (1 + 2 * HG)

        def groups(eng, step):
            step(0, 0, True, False)
            step(1, 1, False, False)
            with eng.Fori(1, G // 2 - 1) as i:
                step(2 * i, 0, False, False)
                step(2 * i + 1, 1, False, False)
            step(G - 2, 0, False, False)
            step(G - 1, 1, False, True)

        def base(eng, g, per_group):
            if isinstance(g, int):
                return g * per_group
            r = eng.alloc_register(f"base{nc.next_id()}")
            eng.reg_mov(r, g * per_group)
            return eng.snap(r, min_val=2 * per_group, max_val=G * per_group)

        with nc.Block() as block:
            @block.sync
            def _(sp):
                def load_qk(g, half, here, loaded):
                    gb = g % GB
                    for part, (kk, qq) in enumerate(((m.k_hi_d, m.q_hi_d), (m.k_lo_d, m.q_hi_d), (m.k_hi_d, m.q_lo_d))):
                        rows = slice(part * DH, (part + 1) * DH)
                        for aug, d in ((k_aug, kk), (q_aug, qq)):
                            sp.dma_start(aug[rows, half, :, here].bitcast(F32),
                                         d[g].rearrange("(h d) n -> d h n", d=DH)[:, :, here]).then_inc(loaded, 16)
                    sp.dma_start(k_aug[ROW_ALIBI:ROWS, half, :, here].bitcast(F32),
                                 m.k_rows_d.rearrange("r (g h) n -> g r h n", h=HG)[gb][:, :, here]).then_inc(loaded, 16)
                    sp.dma_start(q_aug[ROW_ALIBI:ROWS, half, :, here].bitcast(F32), m.q_rows_d[0:4, :, here]).then_inc(loaded, 16)

                def load(g, half):
                    wait_past(sp, pv_done, (g - 1) * NR)
                    if isinstance(g, int) and g == 1:
                        sp.wait_ge(slots_stored, 16 * NT)
                    if isinstance(g, int) and g == 0:
                        for cc in range(QC - 1):
                            load_qk(g, half, slice(cc * CH, (cc + 1) * CH), first_loaded[cc])
                    else:
                        load_qk(g, half, slice(0, S), aug_loaded[half])
                    gb = g % GB
                    v_bg = m.v_d.rearrange("(b j p) (g e) -> b g p j e", b=B, p=P, e=P)
                    sp.dma_start(v_sb[:, half], v_bg[g // GB, gb]).then_inc(v_loaded[half], 16)
                    if isinstance(g, int) and g == 0:
                        load_qk(g, half, slice(S - CH, S), aug_loaded[half])

                def max_rows(g, cc, half):
                    n, here = g * QC + cc, slice(cc * CH, (cc + 1) * CH)
                    sp.wait_ge(max_lo_done, n + 1)
                    sp.dma_start(q_aug[ROW_ALIBI:ROW_MAX, half, :, here].bitcast(F32), m.q_rows_d[4:6, :, here]).then_inc(
                        max_rows_loaded[cc % 2], 16)
                    for row, part in ((ROW_MAX, max_hi), (ROW_MAX + 1, max_lo)):
                        for hh in range(HG):
                            sp.dma_start(q_aug[row:row + 1, half, hh, here].bitcast(F32),
                                         part[hh * TPC:(hh + 1) * TPC, cc % 2].bitcast(F32)).then_inc(max_rows_loaded[cc % 2], 16)

                def y_out(g, cc):
                    sp.wait_ge(y_done, g * QC + cc + 1)
                    sp.dma_start(m.y_d[g, :, cc * CH:(cc + 1) * CH], y_sb[:, cc % 2]).then_inc(y_stored[cc % 2], 16)

                def step(g, half, first, last):
                    if first:
                        max_rows(g, 1, half)
                    elif not last:
                        load(g + 1, 1 - half)
                    else:
                        sp.wait_ge(pv_done, g * NR)
                        for e in range(E):
                            sp.dma_start(m.w_nat[:, 1 - e // (E // 2), e % (E // 2)], m.w_e[e].rearrange("(k p) n -> p k n", p=P)).then_inc(
                                experts_loaded, 16)
                    if first:
                        y_out(g, 0)
                        max_rows(g, 2, half)
                        load(g + 1, 1 - half)
                        y_out(g, 1)
                        max_rows(g, 3, half)
                        max_rows(g + 1, 0, 1 - half)
                        max_rows(g + 1, 1, 1 - half)
                        y_out(g, 2)
                        max_rows(g + 1, 2, 1 - half)
                        return
                    y_out(g - 1, QC - 1)
                    y_out(g, 0)
                    max_rows(g, 3, half)
                    if not last:
                        max_rows(g + 1, 0, 1 - half)
                    y_out(g, 1)
                    if not last:
                        max_rows(g + 1, 1, 1 - half)
                    y_out(g, 2)
                    if last:
                        y_out(g, 3)
                    else:
                        max_rows(g + 1, 2, 1 - half)

                load(0, 0)
                max_rows(0, 0, 0)
                groups(sp, step)
                for s in y_stored:
                    sp.wait_ge(s, 16 * G * QC // 2)
                sp.wait_ge(experts_loaded, 16 * E)

            @block.gpsimd
            def _(pool):
                def bias_of(g, half):
                    wait_past(pool, exp_done, (g - 1) * NSU)
                    nc.gpsimd.tensor_copy(bias[:, half], m.alibi_bias[:, bass.ts(g % GB, HG * QT)]).then_inc(bias_ready, 1)

                bias_of(0, 0)

                xn_t = m.xn_d.rearrange("(n p) d -> p n d", p=P)
                rows_sb = [buffer[:, 1].bitcast(F32).rearrange("p h (n d) -> p (h n) d", d=D) for buffer in (q_aug, k_aug)]

                def load_rows(k):
                    t0 = k * XN_TILES
                    pool.dma_start(rows_sb[t0 // (NT // 2)][:, t0 % (NT // 2):t0 % (NT // 2) + XN_TILES],
                                   xn_t[:, t0:t0 + XN_TILES]).then_inc(xn_loaded[k % 2], 16)

                pool.wait_ge(aug_loaded[0], AUG)
                pool.wait_ge(max_rows_loaded[0], MAX_ROWS)
                load_rows(0)

                def to_slots(k):
                    if k + 1 < NT // XN_TILES:
                        load_rows(k + 1)
                    pool.wait_ge(xn_loaded[k % 2], 16 * (k // 2 + 1))
                    for t in range(k * XN_TILES, (k + 1) * XN_TILES):
                        pool.indirect_dma_start(
                            m.slot_x_d, bass.IndirectOffsetOnAxis(ap=m.slot[:, t:t + 1], axis=0),
                            rows_sb[t // (NT // 2)][:, t % (NT // 2)], None).then_inc(slots_stored, 16)

                pieces = {0: range(0, 3), 1: range(3, 4), 2: range(4, NT // XN_TILES)}

                def normalise(g, cc):
                    n = g * QC + cc
                    pool.wait_ge(inverted, (n + 1) * QUARTERS)
                    nc.gpsimd.tensor_tensor(y_sb[:, cc % 2], y_sb[:, cc % 2], den_sb[:, cc % 2], ALU.mult).then_inc(y_done, 1)

                def step(g, half, first, last):
                    if not last:
                        bias_of(g + 1, 1 - half)
                    exps, used = base(pool, g, NSU), base(pool, g, NPAIR)
                    for p in range(NPAIR + 1):
                        if p in Y_BEFORE_PAIR:
                            back, cc = Y_BEFORE_PAIR[p]
                            if not (first and back):
                                normalise(g - back, cc)
                        if p == NPAIR:
                            break
                        if first:
                            for k in pieces.get(p, []):
                                to_slots(k)
                        r1 = PAIR_LAST[p]
                        s0, s1 = (r1 - 1) % P_SLOTS, r1 % P_SLOTS
                        if not (first and p < 2):
                            pool.wait_ge(pair_used, used + (p - 1))
                        for hh in range(HG):
                            pool.wait_ge(exp_done, exps + (r1 * HG + hh + 1))
                            nc.gpsimd.tensor_tensor(pair_sum[:, p % 2, hh], probs[:, s0, hh], probs[:, s1, hh],
                                                    ALU.add).then_inc(pair_added, 1)

                groups(pool, step)
                normalise(G - 1, QC - 1)

            @block.vector
            def _(dve):
                nc.vector.memset(neg_max[:], 0.0).then_inc(max_blank, 1)
                dve.wait_ge(max_blank, 1)
                part = part_max[:].rearrange("p (h i) k -> p h i k", h=HG)

                def take_max(u, bank, units):
                    i, kc, hh = MAX_UNITS[u]
                    w = min(CH, (i + 1) * P - kc * CH)
                    dve.wait_ge(max_scored, units + (u + 1))
                    nc.vector.tensor_reduce(part_max[:, hh * QT + i, kc:kc + 1], max_ps[:, bank, 0:w], AX.X,
                                            ALU.max).then_inc(max_taken, 1)

                def fold(g, cc, units):
                    n = g * QC + cc
                    dve.wait_ge(max_taken, units + (OF_CHUNK[cc][-1] + 1))
                    nc.vector.tensor_reduce(row_max[:].rearrange("p (h i) -> p h i", h=HG),
                                            part[:, :, cc * TPC:(cc + 1) * TPC, 0:cc + 1], AX.X, ALU.max).then_inc(folded, 1)
                    wait_past(dve, max_turned, n)
                    dve.wait_ge(folded, n + 1)
                    nc.vector.tensor_tensor(neg_max[:, 0:HG * TPC], m.max_shift[:, bass.ts(n % (GB * QC), HG * TPC)], row_max[:],
                                            ALU.subtract).then_inc(neg_done, 1)

                def low_rows(g, cc, bank):
                    dve.wait_ge(max_hi_done, g * QC + cc + 1)
                    nc.vector.tensor_tensor(max_lo[:, cc % 2], max_ps[0:HG * TPC, bank, 0:P], max_hi[:, cc % 2].bitcast(F32),
                                            ALU.subtract).then_inc(max_lo_done, 1)

                def maxima(events, banks, g, units):
                    for dg, kind, n in events:
                        if kind == UNIT:
                            take_max(n, banks[dg, kind, n][0], units[dg])
                        elif kind == FOLD:
                            fold(g + dg, n, units[dg])
                        elif kind == SPLIT:
                            low_rows(g + dg, n, banks[dg, TURN, n][0])

                def invert(g, cc, k):
                    dve.wait_ge(accs_left, g * QC + cc + 1)
                    quarter = den_sb[:, cc % 2, bass.ts(k, CH // QUARTERS)]
                    nc.vector.reciprocal(quarter, quarter).then_inc(inverted, 1)

                def step(g, half, first, last):
                    events, banks = plan_of(g, last)
                    units = base(dve, g, NMU), None if last else base(dve, g + 1, NMU)
                    for r in range(NR):
                        maxima(events[r], banks, g, units)
                        if r in INVERT_AT:
                            back, cc, k = INVERT_AT[r]
                            if not (first and back):
                                invert(g - back, cc, k)

                maxima(PLAN_BEFORE[0], BANKS_BEFORE, 0, (0, None))
                groups(dve, step)
                for k in range(QUARTERS):
                    invert(G - 1, QC - 1, k)

            @block.scalar
            def _(act):
                def maxima(events, banks, g):
                    for dg, kind, n in events:
                        if kind == SPLIT:
                            act.wait_ge(max_turned, (g + dg) * QC + n + 1)
                            wait_past(act, max_rows_loaded[n % 2], MAX_ROWS * ((g + dg) * (QC // 2) + n // 2))
                            nc.scalar.activation(max_hi[:, n % 2], max_ps[0:HG * TPC, banks[dg, TURN, n][0], 0:P],
                                                 ACT.Copy).then_inc(max_hi_done, 1)

                def leave(g, cc):
                    act.wait_ge(pv_done, g * NR + LAST_ROUND[cc] + 1)
                    wait_past(act, y_stored[cc % 2], 16 * (g * (QC // 2) + cc // 2))
                    nc.scalar.activation(acc_sb[:, cc % 2], acc_ps[:], ACT.Copy).then_inc(accs_left, 1)

                def step(g, half, first, last):
                    events, banks = plan_of(g, last)
                    act.wait_ge(bias_ready, g + 1)
                    units, rounds, adds = base(act, g, NSU), base(act, g, NR), base(act, g, NPAIR * HG)
                    for r, (cc, jb) in enumerate(ROUNDS):
                        maxima(events[r], banks, g)
                        off = max(0, jb - TPC * cc) * P
                        back, e = earlier_user(r, P_SLOTS, NR)
                        if not (first and back):
                            act.wait_ge(pv_done, rounds + (e + 1 - back * NR))
                            if e in PAIR_OF:
                                act.wait_ge(pair_added, adds + ((PAIR_OF[e] + 1 - back * NPAIR) * HG))
                        dist = jb - TPC * cc + QT - TPC
                        for hh in range(HG):
                            act.wait_ge(scored, units + (r * HG + hh + 1))
                            nc.scalar.activation(probs[:, r % P_SLOTS, hh, off:CH],
                                                 score_ps[:, (r * HG + hh) % S_BANKS, off:CH], ACT.Exp,
                                                 bias=bias[:, half, hh * QT + dist:hh * QT + dist + 1]).then_inc(exp_done, 1)
                        if r in LEAVE_AT:
                            back, done = LEAVE_AT[r]
                            if not (first and back):
                                leave(g - back, done)

                maxima(PLAN_BEFORE[0], BANKS_BEFORE, 0)
                groups(act, step)
                leave(G - 1, QC - 1)

            @block.tensor
            def _(pe):
                def bank_free(event, g, taken):
                    if event:
                        dg, kind, n = event
                        if kind == UNIT:
                            pe.wait_ge(max_taken, taken[dg] + (n + 1))
                        else:
                            pe.wait_ge(max_lo_done, (g + dg) * QC + n + 1)

                def max_unit(half, u, bank):
                    i, kc, hh = MAX_UNITS[u]
                    w = min(CH, (i + 1) * P - kc * CH)
                    diag = kc == i // TPC
                    last = nc.tensor.matmul(max_ps[:, bank, 0:w], q_aug[0:ROW_MAX, half, hh, i * P:(i + 1) * P],
                                            k_aug[0:ROW_MAX, half, hh, kc * CH:kc * CH + w], start=True, stop=not diag)
                    if diag:
                        last = nc.tensor.matmul(max_ps[:, bank, w - P:w], m.ident_bf[:], m.mask_qk[:], start=False, stop=True)
                    last.then_inc(max_scored, 1)

                def maxima(events, banks, g, half, taken):
                    for dg, kind, n in events:
                        if (dg, kind, n) == (1, UNIT, 0):
                            pe.wait_ge(aug_loaded[1 - half], AUG * ((g + 1) // 2 + 1))
                        if isinstance(g, int) and g == 0 and (dg, kind, n) == (0, UNIT, OF_CHUNK[1][0]):
                            pe.wait_ge(first_loaded[1], AUG)
                        if isinstance(g, int) and g == 0 and (dg, kind, n) == (0, UNIT, OF_CHUNK[QC - 1][0]):
                            pe.wait_ge(aug_loaded[0], AUG)
                        bank, earlier = banks[dg, kind, n]
                        bank_free(earlier, g, taken)
                        if kind == UNIT:
                            max_unit((half + dg) % 2, n, bank)
                        else:
                            pe.wait_ge(neg_done, (g + dg) * QC + n + 1)
                            nc.tensor.transpose(max_ps[:, bank, 0:P], neg_max[:], m.ident[:]).then_inc(max_turned, 1)

                def score_unit(half, r, hh, first, exps):
                    cc, jb = ROUNDS[r]
                    off = max(0, jb - TPC * cc) * P
                    diag = jb >= TPC * cc
                    u = r * HG + hh
                    back, e = earlier_user(u, S_BANKS, NSU)
                    if not (first and back):
                        pe.wait_ge(exp_done, exps + (e + 1 - back * NSU))
                    last = nc.tensor.matmul(score_ps[:, u % S_BANKS, off:CH], k_aug[0:ROWS, half, hh, jb * P:(jb + 1) * P],
                                            q_aug[0:ROWS, half, hh, cc * CH + off:(cc + 1) * CH], start=True, stop=not diag)
                    if diag:
                        last = nc.tensor.matmul(score_ps[:, u % S_BANKS, off:off + P], m.ident_bf[:], m.mask_kq[:],
                                                start=False, stop=True)
                    last.then_inc(scored, 1)

                def pair_product(p, start, adds):
                    for hh in range(HG):
                        pe.wait_ge(pair_added, adds + (p * HG + hh + 1))
                        last = nc.tensor.matmul(den_ps[hh * DH:(hh + 1) * DH, :], m.ones[:], pair_sum[:, p % 2, hh],
                                                start=start, stop=False)
                    last.then_inc(pair_used, 1)

                def probs_of(g, r, exps):
                    cc, jb = ROUNDS[r]
                    if jb == 0:
                        wait_past(pe, accs_left, g * QC + cc)
                    pe.wait_ge(exp_done, exps + (r + 1) * HG)

                def has_row_sums(r):
                    return r not in PAIR_OF or r - 2 in PAIR_LAST.values()

                def row_sums(g, r, exps, adds):
                    cc, jb = ROUNDS[r]
                    off = max(0, jb - TPC * cc) * P
                    probs_of(g, r, exps)
                    if r - 2 in PAIR_LAST.values():
                        pair_product(PAIR_OF[r - 2], ROUNDS[r - 2] == (cc, 1), adds)
                    if r not in PAIR_OF:
                        for hh in range(HG):
                            nc.tensor.matmul(den_ps[hh * DH:(hh + 1) * DH, off:CH], m.ones[:],
                                             probs[:, r % P_SLOTS, hh, off:CH], start=jb == 0, stop=r == LAST_ROUND[cc])

                def value_products(g, half, r, exps):
                    cc, jb = ROUNDS[r]
                    off = max(0, jb - TPC * cc) * P
                    if not has_row_sums(r):
                        probs_of(g, r, exps)
                    for hh in range(HG):
                        last = nc.tensor.matmul(y_ps[hh * DH:(hh + 1) * DH, off:CH],
                                                v_sb[:, half, jb, hh * DH:(hh + 1) * DH],
                                                probs[:, r % P_SLOTS, hh, off:CH], start=jb == 0, stop=r == LAST_ROUND[cc])
                    last.then_inc(pv_done, 1)

                def step(g, half, first, last):
                    if first:
                        pe.wait_ge(first_loaded[2], AUG)
                    pe.wait_ge(v_loaded[half], 16 * (g // 2 + 1))
                    exps, adds = base(pe, g, NSU), base(pe, g, NPAIR * HG)
                    taken = base(pe, g, NMU), None if last else base(pe, g + 1, NMU)
                    plan, banks = plan_of(g, last)
                    for r in range(NR + 1):
                        events = [e for e in plan[r] if e[1] in (UNIT, TURN)] if r < NR else []
                        if r < NR and ROUNDS[r][1] == 0:
                            cc = ROUNDS[r][0]
                            pe.wait_ge(max_rows_loaded[cc % 2], MAX_ROWS * (g * (QC // 2) + cc // 2 + 1))
                        for hh in range(HG):
                            if r < NR:
                                score_unit(half, r, hh, first, exps)
                            if r and hh == HG // 2 and has_row_sums(r - 1):
                                row_sums(g, r - 1, exps, adds)
                            maxima(events[len(events) * hh // HG:len(events) * (hh + 1) // HG], banks, g, half, taken)
                        if r:
                            value_products(g, half, r - 1, exps)

                pe.wait_ge(first_loaded[0], AUG)
                events = [e for e in PLAN_BEFORE[0] if e[1] in (UNIT, TURN)]
                maxima(events, BANKS_BEFORE, 0, 0, (0, None))
                groups(pe, step)


def run_experts(nc, m):
    with ExitStack() as c:
        sb = lambda n, s, d: c.enter_context(nc.sbuf_tensor(n, s, d))
        pb = lambda n, s, d: c.enter_context(nc.psum_tensor(n, s, d))
        sem = lambda n: c.enter_context(nc.semaphore(n))
        wT_hi, wT_lo = (t[:].rearrange("p a h n -> p (a h n)").rearrange("p (e k d) -> p e k d", e=E, k=KC)
                        for t in (m.q_aug, m.k_aug))
        w_nat = [m.w_nat[:, 1, e] for e in range(E // 2)] + [m.w_nat[:, 0, e] for e in range(E // 2)]
        w_order = [*range(E // 2, E), *range(E // 2)]
        bias_all = sb("bias_all", [P, E, D], F32)
        rows = sb("rows", [P, 2, D], F32)
        rT_hi = sb("rT_hi", [P, 2, KC, P], F32R)
        rT_lo = sb("rT_lo", [P, 2, KC, P], F32R)
        y_rows = sb("y_rows", [P, 2, D], F32)
        turn_ps = pb("turn_ps", [P, 8, D], F32)
        prod_ps = turn_ps[:, 2:4]

        b_loaded = sem("b_loaded")
        rows_loaded = [sem("rows_loaded0"), sem("rows_loaded1")]
        turned, hi_done, lo_done = sem("w_turned"), sem("w_hi_done2"), sem("w_lo_done2")
        r_turned, r_hi_done, r_lo_done = sem("r_turned"), sem("r_hi_done"), sem("r_lo_done")
        prod_done, y_done = sem("prod_done"), sem("y_rows_done")
        y_stored = [sem("y_rows_stored0"), sem("y_rows_stored1")]
        wo_loaded, wo_hi_done, wo_lo_done, y_loaded = (
            sem("wo_loaded"), sem("wo_hi_done"), sem("wo_lo_done"), sem("y_loaded"))
        NW = E * KC
        WO_AT = 1

        def is_tile(j, n):
            return isinstance(j, int) and j == n

        def tile_pairs(eng, body):
            body(0, 0, 0, True)
            body(1, 0, 1, True)
            with eng.Fori(1, SLOT_TILES // 2) as i:
                body(2 * i, i, 0, True)
                body(2 * i + 1, i, 1, True)
            body(SLOT_TILES - 1, SLOT_TILES // 2, 0, False)

        with nc.Block() as block:
            x_t = m.slot_x_d.rearrange("(n p) d -> n p d", p=P)
            y_t = m.slot_y_d.rearrange("(n p) d -> n p d", p=P)

            @block.sync
            def _(sp):
                sp.dma_start(bias_all[:], m.b_e.partition_broadcast(P)).then_inc(b_loaded, 16)
                sp.dma_start(rows[:, 0], x_t[0]).then_inc(rows_loaded[0], 16)
                sp.dma_start(rows[:, 1], x_t[1]).then_inc(rows_loaded[1], 16)

                def body(j, i, half, more):
                    if more:
                        sp.wait_ge(r_turned, j + 1)
                        sp.dma_start(rows[:, half], x_t[j + 2]).then_inc(rows_loaded[half], 16)

                tile_pairs(sp, body)
                sp.wait_ge(rows_loaded[1], 16 * (SLOT_TILES // 2 + 1))

            @block.gpsimd
            def _(pool):
                pool.dma_start(m.yT[:, 0], m.w_o.rearrange("(k p) n -> p k n", p=P)).then_inc(wo_loaded, 16)
                pool.dma_start(m.yT[:, 1], y_chunk(m, 1)).then_inc(y_loaded, 16)

                def body(j, i, half, more):
                    pool.wait_ge(y_done, j + 1)
                    pool.dma_start(y_t[j], y_rows[:, half]).then_inc(y_stored[half], 16)
                    if is_tile(j, WO_AT):
                        pool.wait_ge(wo_lo_done, 1)
                        pool.dma_start(m.yT[:, 0], y_chunk(m, 0)).then_inc(y_loaded, 16)

                tile_pairs(pool, body)
                pool.wait_ge(y_loaded, 16 * Y_BUFS)
                pool.wait_ge(y_stored[0], 16 * ((SLOT_TILES + 1) // 2))
                pool.wait_ge(y_stored[1], 16 * (SLOT_TILES // 2))

            @block.scalar
            def _(act):
                for u in range(NW):
                    act.wait_ge(turned, u + 1)
                    nc.scalar.activation(wT_hi[:, w_order[u // KC], u % KC], turn_ps[:, u % 8], ACT.Copy).then_inc(hi_done, 1)

                def high_part(j, half):
                    act.wait_ge(r_turned, j + 1)
                    wait_past(act, prod_done, j - 1)
                    nc.scalar.activation(rT_hi[:, half], turn_ps[:, half].rearrange("p (k n) -> p k n", n=P),
                                         ACT.Copy).then_inc(r_hi_done, 1)

                def body(j, i, half, more):
                    if more:
                        high_part(j + 1, 1 - half)
                    if is_tile(j, WO_AT):
                        act.wait_ge(wo_loaded, 16)
                        nc.scalar.activation(m.wo_hi[:], m.yT[:, 0], ACT.Copy).then_inc(wo_hi_done, 1)

                high_part(0, 0)
                tile_pairs(act, body)

            @block.vector
            def _(dve):
                for u in range(NW):
                    dve.wait_ge(hi_done, u + 1)
                    e = w_order[u // KC]
                    if e < E // 2:
                        dve.wait_ge(turned, (u // KC + 1) * KC)
                    nc.vector.tensor_tensor(wT_lo[:, e, u % KC], turn_ps[:, u % 8], wT_hi[:, e, u % KC].bitcast(F32),
                                            ALU.subtract).then_inc(lo_done, 1)

                def low_part(j, half):
                    dve.wait_ge(r_hi_done, j + 1)
                    nc.vector.tensor_tensor(rT_lo[:, half], turn_ps[:, half].rearrange("p (k n) -> p k n", n=P),
                                            rT_hi[:, half].bitcast(F32), ALU.subtract).then_inc(r_lo_done, 1)

                def body(j, i, half, more):
                    if more:
                        low_part(j + 1, 1 - half)
                    e = dve.value_load(m.tile_expert[0:1, bass.ds(j, 1)], min_val=0, max_val=E - 1)
                    dve.wait_ge(prod_done, j + 1)
                    wait_past(dve, y_stored[half], 16 * i)
                    nc.vector.tensor_tensor(y_rows[:, half], prod_ps[:, half], bias_all[:, e], ALU.add).then_inc(y_done, 1)
                    if is_tile(j, WO_AT):
                        dve.wait_ge(wo_hi_done, 1)
                        nc.vector.tensor_tensor(m.wo_lo[:], m.yT[:, 0], m.wo_hi[:].bitcast(F32),
                                                ALU.subtract).then_inc(wo_lo_done, 1)

                low_part(0, 0)
                dve.wait_ge(b_loaded, 16)
                tile_pairs(dve, body)

            @block.tensor
            def _(pe):
                for u in range(NW):
                    e, k = w_order[u // KC], u % KC
                    if u >= 8:
                        pe.wait_ge(lo_done, u - 7)
                    for a in range(KC):
                        last = nc.tensor.transpose(turn_ps[:, u % 8, a * P:(a + 1) * P],
                                                   w_nat[e][:, a, k * P:(k + 1) * P], m.ident[:])
                    last.then_inc(turned, 1)
                pe.wait_ge(lo_done, NW)

                def turn_rows(j, i, half):
                    pe.wait_ge(rows_loaded[half], 16 * (i + 1))
                    wait_past(pe, r_lo_done, j - 1)
                    for k in range(KC):
                        last = nc.tensor.transpose(turn_ps[:, half, k * P:(k + 1) * P], rows[:, half, k * P:(k + 1) * P],
                                                   m.ident[:])
                    last.then_inc(r_turned, 1)

                def body(j, i, half, more):
                    if more:
                        turn_rows(j + 1, i + half, 1 - half)
                    e = pe.value_load(m.tile_expert[0:1, bass.ds(j, 1)], min_val=0, max_val=E - 1)
                    pe.wait_ge(r_lo_done, j + 1)
                    wait_past(pe, y_done, j - 1)
                    for k in range(KC):
                        for p, (r_part, w_part) in enumerate(((rT_hi, wT_hi), (rT_lo, wT_hi), (rT_hi, wT_lo))):
                            last = nc.tensor.matmul(prod_ps[:, half], r_part[:, half, k], w_part[:, e, k],
                                                    start=(k == 0 and p == 0), stop=(k == KC - 1 and p == 2))
                    last.then_inc(prod_done, 1)

                turn_rows(0, 0, 0)
                tile_pairs(pe, body)


def y_chunk(m, ch):
    return m.y_d.rearrange("(b g) p (c n) -> b c p g n", b=B, n=CH)[ch // QC, ch % QC]


def combine(nc, m):
    BUFS = 4
    with ExitStack() as c:
        sb = lambda n, s, d: c.enter_context(nc.sbuf_tensor(n, s, d))
        pb = lambda n, s, d: c.enter_context(nc.psum_tensor(n, s, d))
        sem = lambda n: c.enter_context(nc.semaphore(n))
        yT_hi = sb("yT_hi", [P, 2, KC, CH], F32R)
        yT_lo = sb("yT_lo", [P, 2, KC, CH], F32R)
        x_sb = sb("x_sb", [P, BUFS, TPC, D], F32)
        e_sb = sb("e_sb", [P, BUFS, TPC, D], F32)
        r_sb = sb("r_sb", [P, TPC, D], F32)
        o_sb = sb("o_sb", [P, 2, TPC, D], F32)
        attn_ps = pb("attn_ps", [P, 2 * TPC, D], F32)

        yT_loaded = [sem(f"yT_loaded{i}") for i in range(Y_BUFS)]
        x_loaded = [sem(f"x2_loaded{i}") for i in range(BUFS)]
        e_loaded = [sem(f"e_loaded{i}") for i in range(BUFS)]
        yT_hi_done, yT_lo_done, attn_done, added, out_done = (
            sem("yT_hi_done"), sem("yT_lo_done"), sem("attn_done"), sem("added"), sem("out_done"))
        out_stored = [sem("out_stored0"), sem("out_stored1")]

        with nc.Block() as block:
            x_c = m.x.rearrange("(c a p) d -> c p a d", a=TPC, p=P)
            o_c = m.out.rearrange("(c a p) d -> c p a d", a=TPC, p=P)

            @block.sync
            def _(sp):
                def load_x(ch):
                    wait_past(sp, added, (ch - BUFS + 1) * TPC)
                    sp.dma_start(x_sb[:, ch % BUFS], x_c[ch]).then_inc(x_loaded[ch % BUFS], 16)

                def load_y(ch):
                    sp.wait_ge(yT_lo_done, ch - Y_BUFS + 1)
                    sp.dma_start(m.yT[:, ch % Y_BUFS], y_chunk(m, ch)).then_inc(yT_loaded[ch % Y_BUFS], 16)

                for ch in range(BUFS - 1):
                    load_x(ch)
                load_y(Y_BUFS)
                for ch in range(NCH):
                    if ch + BUFS - 1 < NCH:
                        load_x(ch + BUFS - 1)
                    if ch + Y_BUFS + 1 < NCH:
                        load_y(ch + Y_BUFS + 1)
                    sp.wait_ge(out_done, (ch + 1) * TPC)
                    sp.dma_start(o_c[ch], o_sb[:, ch % 2]).then_inc(out_stored[ch % 2], 16)
                for s in out_stored:
                    sp.wait_ge(s, 16 * NCH // 2)

            @block.gpsimd
            def _(pool):
                for ch in range(NCH):
                    wait_past(pool, out_done, (ch - BUFS + 1) * TPC)
                    for a in range(TPC):
                        pool.indirect_dma_start(
                            e_sb[:, ch % BUFS, a], None, m.slot_y_d,
                            bass.IndirectOffsetOnAxis(ap=m.slot[:, bass.ds(ch * TPC + a, 1)], axis=0)).then_inc(
                                e_loaded[ch % BUFS], 16)

            @block.scalar
            def _(act):
                for ch in range(NCH):
                    if ch >= Y_BUFS:
                        act.wait_ge(yT_loaded[ch % Y_BUFS], 16 * (ch // Y_BUFS))
                    wait_past(act, attn_done, (ch - 1) * TPC)
                    nc.scalar.activation(yT_hi[:, ch % 2], m.yT[:, ch % Y_BUFS], ACT.Copy).then_inc(yT_hi_done, 1)

            @block.vector
            def _(dve):
                def low_part(ch):
                    dve.wait_ge(yT_hi_done, ch + 1)
                    nc.vector.tensor_tensor(yT_lo[:, ch % 2], m.yT[:, ch % Y_BUFS], yT_hi[:, ch % 2].bitcast(F32),
                                            ALU.subtract).then_inc(yT_lo_done, 1)

                low_part(0)
                low_part(1)
                for ch in range(NCH):
                    dve.wait_ge(x_loaded[ch % BUFS], 16 * (ch // BUFS + 1))
                    for a in range(TPC):
                        n = ch * TPC + a
                        if a == 0:
                            dve.wait_ge(e_loaded[ch % BUFS], 16 * TPC * (ch // BUFS + 1))
                            wait_past(dve, out_stored[ch % 2], 16 * (ch // 2))
                        dve.wait_ge(attn_done, n + 1)
                        nc.vector.tensor_tensor(r_sb[:, a], attn_ps[:, n % (2 * TPC)], x_sb[:, ch % BUFS, a], ALU.add).then_inc(added, 1)
                        dve.wait_ge(added, n + 1)
                        nc.vector.scalar_tensor_tensor(o_sb[:, ch % 2, a], e_sb[:, ch % BUFS, a],
                                                       m.gate[:, bass.ds(n, 1)], r_sb[:, a],
                                                       ALU.mult, ALU.add).then_inc(out_done, 1)
                    if ch + 2 < NCH:
                        low_part(ch + 2)

            @block.tensor
            def _(pe):
                for ch in range(NCH):
                    pe.wait_ge(yT_lo_done, ch + 1)
                    for a in range(TPC):
                        n = ch * TPC + a
                        wait_past(pe, added, n + 1 - 2 * TPC)
                        for k in range(KC):
                            for p, (y_part, w_part) in enumerate(((yT_hi, m.wo_hi), (yT_lo, m.wo_hi), (yT_hi, m.wo_lo))):
                                last = nc.tensor.matmul(attn_ps[:, n % (2 * TPC)], y_part[:, ch % 2, k, a * P:(a + 1) * P],
                                                        w_part[:, k], start=(k == 0 and p == 0), stop=(k == KC - 1 and p == 2))
                        last.then_inc(attn_done, 1)


def kernel(**inputs):
    import concourse.bacc as bacc
    from concourse.bass_utils import run_bass_kernel_spmd

    names = ["L0_attn_x", "L0_attn_W_qkv", "L0_attn_W_o", "L0_ffn_wg", "L0_ffn_W", "L0_ffn_b"]
    nc = bacc.Bacc("TRN2", target_bir_lowering=False, num_devices=1)
    arrays, args = {}, []
    for name in names:
        a = np.ascontiguousarray(inputs[name])
        arrays[f"in_{name}"] = a
        args.append(nc.dram_tensor(f"in_{name}", a.shape, mybir.dt.from_np(a.dtype), kind="ExternalInput").ap())
    args.append(nc.dram_tensor("out_rows", (B, S, D), F32, kind="ExternalOutput").ap())
    prenorm_alibi_attention_plus_top1_experts(nc, *args)
    r = run_bass_kernel_spmd(nc, [arrays], core_ids=[0])
    return r.results[0]["out_rows"]
```
